# Optimizing a Trainium2 kernel written in Bass

```python
import numpy as np
import jax
import jax.numpy as jnp

def _softmax(x, axis=-1):
    return jax.nn.softmax(x, axis=axis)

def _gelu(x):
    return jax.nn.gelu(x, approximate=True)

def _silu(x):
    return jax.nn.silu(x)

def _sigmoid(x):
    return jax.nn.sigmoid(x)

def _layernorm(x, axis=-1, eps=1e-05):
    m = jnp.mean(x, axis=axis, keepdims=True)
    v = jnp.var(x, axis=axis, keepdims=True)
    return (x - m) / jnp.sqrt(v + eps)

def _scatter_add(tgt, idx, src, axis=0):
    return tgt.at[idx].add(src)

def _segment_sum(src, seg, n):
    return jax.ops.segment_sum(src, seg, n)
kernel_name = 'mk_xattn_seq_d4_seqx_r2_4c1af9'

def setup_inputs(seed: int=0):
    np.random.seed(seed)
    _w = jnp.asarray

    def _rec_inputs():
        import jax
        import jax.numpy as jnp
        _rk = jax.random.key(seed)
        x = -0.000125 + 0.9999 * jax.random.normal(jax.random.fold_in(_rk, 1), (8, 512, 512), jnp.float32)
        _lenS = 512 - jax.random.randint(jax.random.fold_in(_rk, 7), (8,), 0, max(1, 512 // 4) + 1, jnp.int32)
        _lenS2 = 512 - jax.random.randint(jax.random.fold_in(_rk, 8), (8,), 0, max(1, 512 // 4) + 1, jnp.int32)
        _ctx_2048P = jax.random.normal(jax.random.fold_in(_rk, 11), (8, 16, 1024), jnp.float32)
        _ctx_2048c = jax.random.dirichlet(jax.random.fold_in(_rk, 511), 0.3 * jnp.ones((16,), jnp.float32), (8, 512))
        _ctx_2048t = jnp.einsum('bsk,bkd->bsd', _ctx_2048c, _ctx_2048P)
        _ctx_2048t = _ctx_2048t * jax.lax.rsqrt(jnp.mean(jnp.square(_ctx_2048t)) + 1e-12) * 0.953939
        ctx_2048 = 5.36139e-06 + 1.00015 * (_ctx_2048t + 0.3 * jax.random.normal(jax.random.fold_in(_rk, 611), (8, 512, 1024), jnp.float32))
        _validS = jnp.arange(512)[None, :] < _lenS[:, None]
        _validS2 = jnp.arange(512)[None, :] < _lenS2[:, None]
        _causal = jnp.tril(jnp.ones((512, 512), dtype=bool))
        mask_S_fk1 = jnp.where(_validS[0], 1.0, 0.0).astype(jnp.float32)
        mask_S_fk0 = jnp.where(_validS[0], 0.0, 1.0).astype(jnp.float32)
        return (x, ctx_2048, mask_S_fk1, mask_S_fk0)
    x, ctx_2048, mask_S_fk1, mask_S_fk0 = _rec_inputs()

    def _L0_xattn_setup():
        import jax, jax.numpy as jnp
        import numpy as np
        HEADS = 16
        HEAD_DIM = 64
        SUPPRESS = 20.0
        key = jax.random.key(seed)
        ks = jax.random.split(key, 8)
        B, HW, C, T, CT = (8, 2048, 512, 77, 1024)
        inner = HEADS * HEAD_DIM
        scale = 0.02
        return {'hidden_states': jax.random.normal(ks[0], (B, HW, C), jnp.float32), 'encoder_hidden_states': jax.random.normal(ks[1], (B, T, CT), jnp.float32), 'mask_A': (jax.random.uniform(ks[2], (HW,)) > 0.5).astype(jnp.float32), 'mask_B': (jax.random.uniform(ks[3], (HW,)) > 0.5).astype(jnp.float32), 'Wq': jax.random.normal(ks[4], (C, inner), jnp.float32) * scale, 'Wk': jax.random.normal(ks[5], (CT, inner), jnp.float32) * scale, 'Wv': jax.random.normal(ks[6], (CT, inner), jnp.float32) * scale, 'Wo': jax.random.normal(ks[7], (inner, C), jnp.float32) * scale, 'bo': jnp.zeros((C,), jnp.float32), 'token_indices_A': jnp.array([2, 3], dtype=jnp.int64), 'token_indices_B': jnp.array([5, 6], dtype=jnp.int64)}
    _L0_xattn_all = _L0_xattn_setup()
    _L0_xattn_in = {k: v for k, v in _L0_xattn_all.items() if k in ('Wq', 'Wk', 'Wv', 'Wo', 'bo', 'token_indices_A', 'token_indices_B')}
    del _L0_xattn_all

    def _L1_xattn_setup():
        import jax, jax.numpy as jnp
        import numpy as np
        D_MODEL = 512
        N_HEADS = 16
        N_KV_HEADS = 4
        HEAD_DIM = D_MODEL // N_HEADS
        SPEAKER_DIM = 1024
        EPS = 1e-05

        def rmsnorm(x, w, eps=EPS):
            xf = x.astype(jnp.float32)
            inv = jax.lax.rsqrt(jnp.mean(xf * xf, axis=-1, keepdims=True) + eps)
            return (xf * inv).astype(x.dtype) * w
        key = jax.random.key(seed)
        ks = jax.random.split(key, 7)
        B, T, S = (4, 1024, 256)
        x = jax.random.normal(ks[0], (B, T, D_MODEL), dtype=jnp.float32)
        cond = jax.random.normal(ks[1], (B, S, SPEAKER_DIM), dtype=jnp.float32)
        sq = 0.02
        wq = jax.random.normal(ks[2], (D_MODEL, N_HEADS * HEAD_DIM), dtype=jnp.float32) * sq
        wk = jax.random.normal(ks[3], (SPEAKER_DIM, N_KV_HEADS * HEAD_DIM), dtype=jnp.float32) * sq
        wv = jax.random.normal(ks[4], (SPEAKER_DIM, N_KV_HEADS * HEAD_DIM), dtype=jnp.float32) * sq
        wo = jax.random.normal(ks[5], (N_HEADS * HEAD_DIM, D_MODEL), dtype=jnp.float32) * sq
        norm_w = jnp.ones((D_MODEL,), dtype=jnp.float32)
        return {'x': x, 'cond': cond, 'wq': wq, 'wk': wk, 'wv': wv, 'wo': wo, 'norm_w': norm_w}
    _L1_xattn_all = _L1_xattn_setup()
    _L1_xattn_in = {k: v for k, v in _L1_xattn_all.items() if k in ('wq', 'wk', 'wv', 'wo', 'norm_w')}
    del _L1_xattn_all

    def _L2_xattn_setup():
        import jax, jax.numpy as jnp
        import numpy as np
        D_MODEL = 512
        N_HEADS = 16
        N_KV_HEADS = 4
        HEAD_DIM = D_MODEL // N_HEADS
        SPEAKER_DIM = 1024
        EPS = 1e-05

        def rmsnorm(x, w, eps=EPS):
            xf = x.astype(jnp.float32)
            inv = jax.lax.rsqrt(jnp.mean(xf * xf, axis=-1, keepdims=True) + eps)
            return (xf * inv).astype(x.dtype) * w
        key = jax.random.key(seed)
        ks = jax.random.split(key, 7)
        B, T, S = (4, 1024, 256)
        x = jax.random.normal(ks[0], (B, T, D_MODEL), dtype=jnp.float32)
        cond = jax.random.normal(ks[1], (B, S, SPEAKER_DIM), dtype=jnp.float32)
        sq = 0.02
        wq = jax.random.normal(ks[2], (D_MODEL, N_HEADS * HEAD_DIM), dtype=jnp.float32) * sq
        wk = jax.random.normal(ks[3], (SPEAKER_DIM, N_KV_HEADS * HEAD_DIM), dtype=jnp.float32) * sq
        wv = jax.random.normal(ks[4], (SPEAKER_DIM, N_KV_HEADS * HEAD_DIM), dtype=jnp.float32) * sq
        wo = jax.random.normal(ks[5], (N_HEADS * HEAD_DIM, D_MODEL), dtype=jnp.float32) * sq
        norm_w = jnp.ones((D_MODEL,), dtype=jnp.float32)
        return {'x': x, 'cond': cond, 'wq': wq, 'wk': wk, 'wv': wv, 'wo': wo, 'norm_w': norm_w}
    _L2_xattn_all = _L2_xattn_setup()
    _L2_xattn_in = {k: v for k, v in _L2_xattn_all.items() if k in ('wq', 'wk', 'wv', 'wo', 'norm_w')}
    del _L2_xattn_all

    def _L3_xattn_setup():
        import jax, jax.numpy as jnp
        import numpy as np
        D_MODEL = 512
        N_HEADS = 16
        N_KV_HEADS = 4
        HEAD_DIM = D_MODEL // N_HEADS
        SPEAKER_DIM = 1024
        EPS = 1e-05

        def rmsnorm(x, w, eps=EPS):
            xf = x.astype(jnp.float32)
            inv = jax.lax.rsqrt(jnp.mean(xf * xf, axis=-1, keepdims=True) + eps)
            return (xf * inv).astype(x.dtype) * w
        key = jax.random.key(seed)
        ks = jax.random.split(key, 7)
        B, T, S = (4, 1024, 256)
        x = jax.random.normal(ks[0], (B, T, D_MODEL), dtype=jnp.float32)
        cond = jax.random.normal(ks[1], (B, S, SPEAKER_DIM), dtype=jnp.float32)
        sq = 0.02
        wq = jax.random.normal(ks[2], (D_MODEL, N_HEADS * HEAD_DIM), dtype=jnp.float32) * sq
        wk = jax.random.normal(ks[3], (SPEAKER_DIM, N_KV_HEADS * HEAD_DIM), dtype=jnp.float32) * sq
        wv = jax.random.normal(ks[4], (SPEAKER_DIM, N_KV_HEADS * HEAD_DIM), dtype=jnp.float32) * sq
        wo = jax.random.normal(ks[5], (N_HEADS * HEAD_DIM, D_MODEL), dtype=jnp.float32) * sq
        norm_w = jnp.ones((D_MODEL,), dtype=jnp.float32)
        return {'x': x, 'cond': cond, 'wq': wq, 'wk': wk, 'wv': wv, 'wo': wo, 'norm_w': norm_w}
    _L3_xattn_all = _L3_xattn_setup()
    _L3_xattn_in = {k: v for k, v in _L3_xattn_all.items() if k in ('wq', 'wk', 'wv', 'wo', 'norm_w')}
    del _L3_xattn_all
    return {'x': x, 'ctx_2048': ctx_2048, 'mask_S_fk1': mask_S_fk1, 'mask_S_fk0': mask_S_fk0, 'L0_xattn_Wq': _L0_xattn_in['Wq'], 'L0_xattn_Wk': _L0_xattn_in['Wk'], 'L0_xattn_Wv': _L0_xattn_in['Wv'], 'L0_xattn_Wo': _L0_xattn_in['Wo'], 'L0_xattn_bo': _L0_xattn_in['bo'], 'L0_xattn_token_indices_A': _L0_xattn_in['token_indices_A'], 'L0_xattn_token_indices_B': _L0_xattn_in['token_indices_B'], 'L1_xattn_wq': _L1_xattn_in['wq'], 'L1_xattn_wk': _L1_xattn_in['wk'], 'L1_xattn_wv': _L1_xattn_in['wv'], 'L1_xattn_wo': _L1_xattn_in['wo'], 'L1_xattn_norm_w': _L1_xattn_in['norm_w'], 'L2_xattn_wq': _L2_xattn_in['wq'], 'L2_xattn_wk': _L2_xattn_in['wk'], 'L2_xattn_wv': _L2_xattn_in['wv'], 'L2_xattn_wo': _L2_xattn_in['wo'], 'L2_xattn_norm_w': _L2_xattn_in['norm_w'], 'L3_xattn_wq': _L3_xattn_in['wq'], 'L3_xattn_wk': _L3_xattn_in['wk'], 'L3_xattn_wv': _L3_xattn_in['wv'], 'L3_xattn_wo': _L3_xattn_in['wo'], 'L3_xattn_norm_w': _L3_xattn_in['norm_w']}

def reference(x, ctx_2048, mask_S_fk1, mask_S_fk0, L0_xattn_Wq, L0_xattn_Wk, L0_xattn_Wv, L0_xattn_Wo, L0_xattn_bo, L0_xattn_token_indices_A, L0_xattn_token_indices_B, L1_xattn_wq, L1_xattn_wk, L1_xattn_wv, L1_xattn_wo, L1_xattn_norm_w, L2_xattn_wq, L2_xattn_wk, L2_xattn_wv, L2_xattn_wo, L2_xattn_norm_w, L3_xattn_wq, L3_xattn_wk, L3_xattn_wv, L3_xattn_wo, L3_xattn_norm_w):
    import jax
    import jax.numpy as jnp

    def _L0_xattn_ref(hidden_states, encoder_hidden_states, mask_A, mask_B, Wq, Wk, Wv, Wo, bo, token_indices_A, token_indices_B):
        import jax, jax.numpy as jnp
        import numpy as np
        HEADS = 16
        HEAD_DIM = 64
        SUPPRESS = 20.0
        B, HW, C = hidden_states.shape
        T = encoder_hidden_states.shape[1]
        residual = hidden_states
        q = hidden_states @ Wq
        k = encoder_hidden_states @ Wk
        v = encoder_hidden_states @ Wv
        q = q.reshape(B, HW, HEADS, HEAD_DIM).transpose(0, 2, 1, 3)
        k = k.reshape(B, T, HEADS, HEAD_DIM).transpose(0, 2, 1, 3)
        v = v.reshape(B, T, HEADS, HEAD_DIM).transpose(0, 2, 1, 3)
        scale = HEAD_DIM ** (-0.5)
        logits = jnp.einsum('bhqd,bhkd->bhqk', q, k) * scale
        suppress_A_in = 1.0 - mask_A
        suppress_B_in = 1.0 - mask_B
        col_bias = jnp.zeros((HW, T), logits.dtype)
        col_bias = col_bias.at[:, token_indices_A].set((-SUPPRESS * suppress_A_in)[:, None])
        col_bias = col_bias.at[:, token_indices_B].set((-SUPPRESS * suppress_B_in)[:, None])
        logits = logits + col_bias[None, None, :, :]
        probs = jax.nn.softmax(logits, axis=-1)
        out = jnp.einsum('bhqk,bhkd->bhqd', probs, v)
        out = out.transpose(0, 2, 1, 3).reshape(B, HW, HEADS * HEAD_DIM)
        out = out @ Wo + bo
        out = out + residual
        return out

    def _L1_xattn_ref(x, cond, wq, wk, wv, wo, norm_w):
        import jax, jax.numpy as jnp
        import numpy as np
        D_MODEL = 512
        N_HEADS = 16
        N_KV_HEADS = 4
        HEAD_DIM = D_MODEL // N_HEADS
        SPEAKER_DIM = 1024
        EPS = 1e-05

        def rmsnorm(x, w, eps=EPS):
            xf = x.astype(jnp.float32)
            inv = jax.lax.rsqrt(jnp.mean(xf * xf, axis=-1, keepdims=True) + eps)
            return (xf * inv).astype(x.dtype) * w
        B, T, _ = x.shape
        S = cond.shape[1]
        n_rep = N_HEADS // N_KV_HEADS
        residual = x
        xn = rmsnorm(x, norm_w)
        q = (xn @ wq).reshape(B, T, N_HEADS, HEAD_DIM)
        k = (cond @ wk).reshape(B, S, N_KV_HEADS, HEAD_DIM)
        v = (cond @ wv).reshape(B, S, N_KV_HEADS, HEAD_DIM)
        qg = q.reshape(B, T, N_KV_HEADS, n_rep, HEAD_DIM)
        scale = 1.0 / np.sqrt(HEAD_DIM).astype(np.float32)
        scores = jnp.einsum('btgrd,bsgd->bgrts', qg, k) * scale
        attn = jax.nn.softmax(scores.astype(jnp.float32), axis=-1).astype(q.dtype)
        out = jnp.einsum('bgrts,bsgd->btgrd', attn, v).reshape(B, T, N_HEADS * HEAD_DIM)
        return residual + out @ wo

    def _L2_xattn_ref(x, cond, wq, wk, wv, wo, norm_w):
        import jax, jax.numpy as jnp
        import numpy as np
        D_MODEL = 512
        N_HEADS = 16
        N_KV_HEADS = 4
        HEAD_DIM = D_MODEL // N_HEADS
        SPEAKER_DIM = 1024
        EPS = 1e-05

        def rmsnorm(x, w, eps=EPS):
            xf = x.astype(jnp.float32)
            inv = jax.lax.rsqrt(jnp.mean(xf * xf, axis=-1, keepdims=True) + eps)
            return (xf * inv).astype(x.dtype) * w
        B, T, _ = x.shape
        S = cond.shape[1]
        n_rep = N_HEADS // N_KV_HEADS
        residual = x
        xn = rmsnorm(x, norm_w)
        q = (xn @ wq).reshape(B, T, N_HEADS, HEAD_DIM)
        k = (cond @ wk).reshape(B, S, N_KV_HEADS, HEAD_DIM)
        v = (cond @ wv).reshape(B, S, N_KV_HEADS, HEAD_DIM)
        qg = q.reshape(B, T, N_KV_HEADS, n_rep, HEAD_DIM)
        scale = 1.0 / np.sqrt(HEAD_DIM).astype(np.float32)
        scores = jnp.einsum('btgrd,bsgd->bgrts', qg, k) * scale
        attn = jax.nn.softmax(scores.astype(jnp.float32), axis=-1).astype(q.dtype)
        out = jnp.einsum('bgrts,bsgd->btgrd', attn, v).reshape(B, T, N_HEADS * HEAD_DIM)
        return residual + out @ wo

    def _L3_xattn_ref(x, cond, wq, wk, wv, wo, norm_w):
        import jax, jax.numpy as jnp
        import numpy as np
        D_MODEL = 512
        N_HEADS = 16
        N_KV_HEADS = 4
        HEAD_DIM = D_MODEL // N_HEADS
        SPEAKER_DIM = 1024
        EPS = 1e-05

        def rmsnorm(x, w, eps=EPS):
            xf = x.astype(jnp.float32)
            inv = jax.lax.rsqrt(jnp.mean(xf * xf, axis=-1, keepdims=True) + eps)
            return (xf * inv).astype(x.dtype) * w
        B, T, _ = x.shape
        S = cond.shape[1]
        n_rep = N_HEADS // N_KV_HEADS
        residual = x
        xn = rmsnorm(x, norm_w)
        q = (xn @ wq).reshape(B, T, N_HEADS, HEAD_DIM)
        k = (cond @ wk).reshape(B, S, N_KV_HEADS, HEAD_DIM)
        v = (cond @ wv).reshape(B, S, N_KV_HEADS, HEAD_DIM)
        qg = q.reshape(B, T, N_KV_HEADS, n_rep, HEAD_DIM)
        scale = 1.0 / np.sqrt(HEAD_DIM).astype(np.float32)
        scores = jnp.einsum('btgrd,bsgd->bgrts', qg, k) * scale
        attn = jax.nn.softmax(scores.astype(jnp.float32), axis=-1).astype(q.dtype)
        out = jnp.einsum('bgrts,bsgd->btgrd', attn, v).reshape(B, T, N_HEADS * HEAD_DIM)
        return residual + out @ wo
    x = _L0_xattn_ref(x, ctx_2048, mask_S_fk1, mask_S_fk0, L0_xattn_Wq, L0_xattn_Wk, L0_xattn_Wv, L0_xattn_Wo, L0_xattn_bo, L0_xattn_token_indices_A, L0_xattn_token_indices_B)
    x = _L1_xattn_ref(x, ctx_2048, L1_xattn_wq, L1_xattn_wk, L1_xattn_wv, L1_xattn_wo, L1_xattn_norm_w)
    x = _L2_xattn_ref(x, ctx_2048, L2_xattn_wq, L2_xattn_wk, L2_xattn_wv, L2_xattn_wo, L2_xattn_norm_w)
    x = _L3_xattn_ref(x, ctx_2048, L3_xattn_wq, L3_xattn_wk, L3_xattn_wv, L3_xattn_wo, L3_xattn_norm_w)
    return x

_drawn_inputs = setup_inputs


def setup_inputs(seed=0):
    import zlib

    import numpy as np

    out = dict(_drawn_inputs(seed))
    spreads = {'L0_xattn_bo': (0.0, 0.1),
     'L1_xattn_norm_w': (1.0, 0.6),
     'L2_xattn_norm_w': (1.0, 0.6),
     'L3_xattn_norm_w': (1.0, 0.6)}
    factors = {'mask_S_fk1': 8.0,
     'mask_S_fk0': 8.0,
     'L0_xattn_Wq': 3.048,
     'L0_xattn_Wk': 3.035,
     'L1_xattn_wq': 4.115,
     'L1_xattn_wk': 4.103,
     'L2_xattn_wq': 4.115,
     'L2_xattn_wk': 4.105,
     'L3_xattn_wq': 4.151,
     'L3_xattn_wk': 4.144}
    for name, (base, spread) in spreads.items():
        noise = np.random.default_rng([zlib.crc32(name.encode()), seed]).standard_normal(out[name].shape)
        drawn = base * np.exp(spread * noise) if base else spread * noise
        out[name] = jnp.asarray(drawn.astype(out[name].dtype))
    for name, factor in factors.items():
        out[name] = (out[name] * factor).astype(out[name].dtype)
    return out
```

```python
from contextlib import ExitStack, contextmanager

import concourse.bass as bass
from concourse import mybir

P = 128
W = 512
F32 = mybir.dt.float32
F32R = mybir.dt.float32r
I32 = mybir.dt.int32
ALU = mybir.AluOpType
ACT = mybir.ActivationFunctionType
AX = mybir.AxisListType

B = 8
C = 512
CT = 1024
S = 512
INNER0 = 1024
INNER = 512
KV = 128
LAYERS = 3
PROJ = INNER0 + LAYERS * KV
KT = S // P
QT = S // P
CK = C // P
EPS = 1e-5
SUPPRESS = 20.0
DMA = 16
SHIFT = 96
BIAS = 64



def as_f32(ap):
    return ap.bitcast(F32)


def project_context(nc, name, ctx_t, weights, scratch, is_k):
    KC = CT // P
    VP = 3
    WB = PROJ // P if is_k else KT * VP
    NCH = KC // 2
    CHUNK_AT = {2 * j + 1: j for j in range(NCH)}
    with ExitStack() as mem:
        def sb(n, shape, dt):
            return mem.enter_context(nc.sbuf_tensor(f"{name}_{n}", shape, dt))

        def sem(n):
            return mem.enter_context(nc.semaphore(f"{name}_{n}"))

        w_hi = sb("w_hi", [P, KC, PROJ], F32R)
        w_lo = sb("w_lo", [P, KC, PROJ], F32R)
        c_hi = [sb(f"c_hi{i}", [P, KC, S], F32R) for i in range(2)]
        c_lo = [sb(f"c_lo{i}", [P, KC, S], F32R) for i in range(2)]
        raw = sb("raw", [P, 2, PROJ], F32)
        out = [sb(f"out{i}", [P, 2, W], F32R) if is_k else sb(f"out{i}", [P, 1, W], F32) for i in range(2)]
        ps = mem.enter_context(nc.psum_tensor(f"{name}_ps", [P, 2, W], F32))

        raw_in = [sem(f"raw_in{i}") for i in range(2)]
        hi_done = sem("hi_done")
        lo_done = sem("lo_done")
        block_done = sem("block_done")
        out_hi = sem("out_hi")
        out_lo = sem("out_lo")
        stored = [sem(f"stored{i}") for i in range(2)]

        w_rows = weights.rearrange("(k p) n -> p k n", p=P)
        taken = out_lo if is_k else out_hi

        def chunk_view(j):
            return raw[:, j % 2, 0:2 * S].rearrange("p (k s) -> p k s", k=2)

        def width(n):
            return W if is_k or n % VP < 2 else LAYERS * KV

        def raw_count(b, j):
            return b * (DMA * NCH // 2) + DMA * (KC // 2 + j // 2 + 1)

        block = mem.enter_context(nc.Block())

        @block.gpsimd
        def _(pool):
            for credit in (taken, *stored):
                pool.sem_inc(credit, 1)

        @block.sync
        def _(sp):
            def load(b, place, j):
                sp.wait_ge(lo_done, place * NCH + KC + j - 1)
                src = ctx_t[b].rearrange("(k p) s -> p k s", p=P)
                sp.dma_start(chunk_view(j), src[:, 2 * j:2 * j + 2, :]).then_inc(raw_in[j % 2], DMA)

            for k in range(KC):
                if k >= 2:
                    sp.wait_ge(lo_done, k - 1)
                sp.dma_start(raw[:, k % 2, :], w_rows[:, k, :]).then_inc(raw_in[k % 2], DMA)
            for j in range(NCH):
                load(0, 0, j)
            with sp.Fori(0, B // 2) as bb:
                for par in range(2):
                    b = bb * 2 + par
                    for n in range(WB):
                        m = par * WB + n
                        sp.wait_ge(taken, 1 + b * WB + n + 1)
                        if is_k:
                            dst = scratch[b, n].rearrange("c p s -> p c s")
                        else:
                            dst = scratch[b, n // VP][:, (n % VP) * W:(n % VP) * W + width(n)]\
                                .rearrange("p (c s) -> p c s", c=1)
                        src = out[m % 2][:, :, 0:width(n)]
                        sp.dma_start(dst, as_f32(src) if is_k else src).then_inc(stored[m % 2], DMA)
                        if n in CHUNK_AT:
                            load((b + 1) % B, b + 1, CHUNK_AT[n])
            for i in range(2):
                sp.wait_ge(stored[i], 1 + DMA * WB * B // 2)

        @block.scalar
        def _(act):
            def round_chunk(place, par, j):
                act.wait_ge(raw_in[j % 2], raw_count(place, j))
                act.activation(c_hi[par][:, 2 * j:2 * j + 2, :], chunk_view(j), ACT.Copy).then_inc(hi_done, 1)

            for k in range(KC):
                act.wait_ge(raw_in[k % 2], DMA * (k // 2 + 1))
                act.activation(w_hi[:, k, :], raw[:, k % 2, :], ACT.Copy).then_inc(hi_done, 1)
            for j in range(NCH):
                round_chunk(0, 0, j)
            with act.Fori(0, B // 2) as bb:
                for par in range(2):
                    b = bb * 2 + par
                    for n in range(WB):
                        m = par * WB + n
                        w = width(n)
                        act.wait_ge(block_done, b * WB + n + 1)
                        act.wait_ge(stored[m % 2], 1 + bb * (DMA * WB) + DMA * (m // 2))
                        act.activation(out[m % 2][:, 0, 0:w], ps[:, m % 2, 0:w], ACT.Copy).then_inc(out_hi, 1)
                        if n in CHUNK_AT:
                            round_chunk(b + 1, 1 - par, CHUNK_AT[n])

        @block.vector
        def _(dve):
            def rest_chunk(place, par, j):
                dve.wait_ge(hi_done, place * NCH + KC + j + 1)
                dve.tensor_tensor(c_lo[par][:, 2 * j:2 * j + 2, :], chunk_view(j),
                                  as_f32(c_hi[par][:, 2 * j:2 * j + 2, :]), ALU.subtract).then_inc(lo_done, 1)

            for k in range(KC):
                dve.wait_ge(hi_done, k + 1)
                dve.tensor_tensor(w_lo[:, k, :], raw[:, k % 2, :], as_f32(w_hi[:, k, :]), ALU.subtract)\
                    .then_inc(lo_done, 1)
            for j in range(NCH):
                rest_chunk(0, 0, j)
            with dve.Fori(0, B // 2) as bb:
                for par in range(2):
                    b = bb * 2 + par
                    for n in range(WB):
                        m = par * WB + n
                        if is_k:
                            dve.wait_ge(out_hi, b * WB + n + 1)
                            dve.tensor_tensor(out[m % 2][:, 1, :], ps[:, m % 2, :], as_f32(out[m % 2][:, 0, :]),
                                              ALU.subtract).then_inc(out_lo, 1)
                        if n in CHUNK_AT:
                            rest_chunk(b + 1, 1 - par, CHUNK_AT[n])

        @block.tensor
        def _(pe):
            with pe.Fori(0, B // 2) as bb:
                for par in range(2):
                    b = bb * 2 + par
                    pe.wait_ge(lo_done, (b + 1) * NCH + KC)
                    for n in range(WB):
                        m = par * WB + n
                        if par == 0 and n < 2:
                            pe.wait_ge(taken, 1 + b * WB)
                        else:
                            pe.wait_ge(taken, 1 + b * WB + n - 1)
                        for k in range(KC):
                            if is_k:
                                pairs = [(w, c[par][:, k, :]) for w, c in ((w_hi, c_hi), (w_hi, c_lo), (w_lo, c_hi))]
                                pairs = [(w[:, k, n * P:(n + 1) * P], c) for w, c in pairs]
                            else:
                                t, c0 = n // VP, (n % VP) * W
                                pairs = [(c[par][:, k, t * P:(t + 1) * P], w[:, k, c0:c0 + width(n)])
                                         for c, w in ((c_hi, w_hi), (c_hi, w_lo), (c_lo, w_hi))]
                            for i, (stationary, moving) in enumerate(pairs):
                                last = pe.matmul(ps[:, m % 2, 0:width(n)], stationary, moving,
                                                 start=(k == 0 and i == 0), stop=(k == KC - 1 and i == 2))
                        last.then_inc(block_done, 1)


class Kind:

    def __init__(self, layers, inner, head, shared_kv, p_slots):
        self.layers = layers
        self.d = head
        self.T = inner // P
        self.H = P // head
        self.shared = shared_kv
        self.NB = 4
        self.PASS = self.NB * head // P
        self.NS = self.H // 2 * KT
        self.M = self.H * QT
        self.KHEADS = 1 if shared_kv else self.H
        self.PS = p_slots
        assert self.NS % p_slots == 0 and self.M == 2 * self.NS and self.T % 2 == 0


def attention_layers(nc, name, kind, x_in, x_out, k_scratch, v_scratch, wq, wo, norm_w=None, bias=None):
    L, d, T, H, NS, M, PASS = kind.layers, kind.d, kind.T, kind.H, kind.NS, kind.M, kind.PASS
    RING = 3
    WCH = 2 * T * P * CK // (4 * W)
    has_norm = norm_w is not None
    scale = d ** -0.5
    uses = [len(range(s, T, RING)) for s in range(RING)]
    with ExitStack() as mem:
        def sb(n, shape, dt):
            return mem.enter_context(nc.sbuf_tensor(f"{name}_{n}", shape, dt))

        def sem(n):
            return mem.enter_context(nc.semaphore(f"{name}_{n}"))

        wq_hi = sb("wq_hi", [P, CK, T * P], F32R)
        wq_lo = sb("wq_lo", [P, CK, T * P], F32R)
        wo_hi = sb("wo_hi", [P, T, C], F32R)
        wo_lo = sb("wo_lo", [P, T, C], F32R)
        x_raw = sb("x_raw", [P, CK, S], F32)
        x_hi = sb("x_hi", [P, CK, S], F32R)
        x_lo = sb("x_lo", [P, CK, S], F32R)
        a_hi = sb("a_hi", [P, T, S], F32R)
        a_lo = sb("a_lo", [P, T, S], F32R)
        q_ops = sb("q_ops", [P, RING, H, PASS, S], F32R)
        k_ops = sb("k_ops", [P, RING, kind.KHEADS, PASS, S], F32R)
        VR = 1 if kind.shared else 2
        v = sb("v", [P, VR, KT, P], F32)
        probs = sb("probs", [P, kind.PS, 2, S], F32)
        stage = sb("stage", [P, 2, S], F32)
        recip = sb("recip", [P, S], F32)
        max_cols = sb("max_cols", [P, QT, P], F32)
        ident = sb("ident", [P, P], F32)
        ones = sb("ones", [P, P], F32)
        if has_norm:
            inv = sb("inv", [P, S], F32)
            sq = sb("sq", [P, 2, S], F32)
            ms = sb("ms", [P, 2, S], F32)
            nw = sb("nw", [P, CK], F32)
        else:
            bo_cols = sb("bo_cols", [P, C // P], F32)
            tok_i = sb("tok_i", [1, 4], I32)
            tok = sb("tok", [1, 4], F32)
            tok_w = sb("tok_w", [1, 4], F32)
            spare = probs[:, 0:4].rearrange("p a c s -> p (a c) s")
            hit = spare[0:1, 0:4, :]
            mrow, brow = spare[0:2, 4, :], spare[0:2, 5, :]
            key_no, key_no_i = spare[0:1, 6, :], spare[0:1, 7, :].bitcast(I32)
            b_hi, b_lo = recip[0:2, :].bitcast(F32R), stage[0:2, 0, :].bitcast(F32R)
            ind = [stage[0:1, 1, :].bitcast(F32R), hit[:, 3, :].bitcast(F32R)]
        ps = mem.enter_context(nc.psum_tensor(f"{name}_ps", [P, 8, W], F32))
        MAXB, OUTB, DENB = (5, 4), 6, 7
        Q_BANK = (4, 6, 7, 5)
        w_raw = probs[:, 0:4].rearrange("p (a b) c s -> p a (b c s)", a=2)
        x_res = probs[:, 0:2].rearrange("p a c s -> p (a c) s")

        consts = sem("consts")
        consts_v = sem("consts_v")
        rows_in = sem("rows_in")
        bias_rows = sem("bias_rows")
        rows_set = sem("rows_set")
        w_in = [sem(f"w_in{i}") for i in range(2)]
        nw_in = sem("nw_in")
        w_rounded = sem("w_rounded")
        w_split = sem("w_split")
        x_in_s = sem("x_in")
        res_in = sem("res_in")
        x_split = sem("x_split")
        x_hi_done = sem("x_hi_done")
        brow_step = sem("brow_step")
        sq_step = sem("sq_step")
        ssum_done = sem("ssum_done")
        ms_step = sem("ms_step")
        inv_done = sem("inv_done")
        q_proj = sem("q_proj")
        q_taken = sem("q_taken")
        q_hi = sem("q_hi")
        q_lo = sem("q_lo")
        q_in = [sem(f"q_in{i}") for i in range(RING)]
        k_in = [sem(f"k_in{i}") for i in range(RING)]
        v_in = [sem(f"v_in{i}") for i in range(VR)]
        smax = sem("smax")
        reduced = sem("reduced")
        turned = sem("turned")
        shifted = sem("shifted")
        scored = sem("scored")
        exped = sem("exped")
        pv = sem("pv")
        recip_done = sem("recip_done")
        normed = sem("normed")
        o_hi = sem("o_hi")
        o_lo = sem("o_lo")
        o_proj = sem("o_proj")
        added = sem("added")
        stored = [sem(f"stored{i}") for i in range(2)]

        @contextmanager
        def layers(eng):
            if L == 1:
                yield 0
            else:
                with eng.Fori(0, L) as l:
                    yield l

        def bank(i):
            return ps[:, i, :]

        def k_head(h):
            return 0 if kind.shared else h

        def rows(p):
            return SHIFT if p == PASS - 1 else P

        block = mem.enter_context(nc.Block())
        X0 = P - d

        @block.sync
        def _(sp):
            if not has_norm:
                sp.dma_start(bo_cols[:, :], bias["bo"]).then_inc(rows_in, DMA)
                for i, m in enumerate(("mask_a", "mask_b")):
                    sp.dma_start(spare[i:i + 1, 4, :], bias[m].rearrange("(a s) -> a s", a=1)).then_inc(rows_in, DMA)
                for i, m in enumerate(("tok_a", "tok_b")):
                    sp.dma_start(tok_i[:, 2 * i:2 * i + 2], bias[m].rearrange("(a s) -> a s", a=1))\
                        .then_inc(rows_in, DMA)
            sp.dma_start(x_raw[:, :, :], x_in[0].rearrange("(k p) s -> p k s", p=P)).then_inc(x_in_s, DMA)
            if not has_norm:
                sp.wait_ge(bias_rows, 6)
                sp.wait_ge(consts_v, 4)
                for s in range(RING):
                    for h in range(H):
                        q_row = as_f32(q_ops[:, s, h, PASS - 1, :])
                        k_row = as_f32(k_ops[:, s, h, PASS - 1, :])
                        sp.dma_start(q_row[BIAS:BIAS + 2, :], as_f32(b_hi)).then_inc(rows_set, DMA)
                        sp.dma_start(q_row[BIAS + 2:BIAS + 4, :], as_f32(b_lo)).then_inc(rows_set, DMA)
                        for r in range(4):
                            sp.dma_start(k_row[BIAS + r:BIAS + r + 1, :], as_f32(ind[r % 2])).then_inc(rows_set, DMA)
                sp.wait_ge(rows_set, 6 * H * RING * DMA)
            with layers(sp) as l:
                sp.wait_ge(added, 1 + l * (B * CK))
                if has_norm:
                    sp.dma_start(nw[:, :], norm_w[l]).then_inc(nw_in, DMA)
                for c in range(WCH):
                    if c >= 2:
                        sp.wait_ge(w_split, l * WCH + c - 1)
                    half = WCH // 2
                    src = (wq[l] if c < half else wo[l]).rearrange("(k p) n -> p k n", p=P)
                    n = src.shape[1] // half
                    src = src[:, (c % half) * n:(c % half + 1) * n, :]
                    dst = w_raw[:, c % 2, :].rearrange("p (k n) -> p k n", k=n)
                    sp.dma_start(dst, src).then_inc(w_in[c % 2], DMA)
                with sp.Fori(0, B) as b:
                    it = b if L == 1 else l * B + b
                    for t in range(T):
                        s = t % RING
                        sp.wait_ge(scored, 1 + it * (T * NS) + max(t - RING + 1, 0) * NS)
                        for i, part in enumerate((0, 1, 0)):
                            at = (i * d) % P
                            dst = as_f32(k_ops[at:at + d, s, :, (i * d) // P, :])
                            if kind.shared:
                                src = k_scratch[b, INNER0 // P + l, part][t * d:(t + 1) * d, :]
                                src = src.rearrange("(h p) s -> p h s", h=1)
                            else:
                                src = k_scratch[b, t, part].rearrange("(h p) s -> p h s", h=H)
                            sp.dma_start(dst, src).then_inc(k_in[s], DMA)
                        if kind.shared and t == 0:
                            sp.wait_ge(pv, 1 + it * (T * KT))
                            src = v_scratch[b].rearrange("k p n -> p k n")
                            sp.dma_start(v[:, 0], src[:, :, bass.ds(INNER0 + l * KV, KV)]).then_inc(v_in[0], DMA)
                        if not kind.shared:
                            sp.wait_ge(pv, 1 + it * (T * KT) + max(t - VR + 1, 0) * KT)
                            src = v_scratch[b].rearrange("k p n -> p k n")
                            sp.dma_start(v[:, t % VR], src[:, :, t * P:(t + 1) * P]).then_inc(v_in[t % VR], DMA)
                        sp.wait_ge(q_lo, it * T + t + 1)
                        for h in range(H):
                            for i, part in enumerate((a_hi, a_hi, a_lo)):
                                at = (i * d) % P
                                sp.dma_start(as_f32(q_ops[at:at + d, s, h, (i * d) // P, :]),
                                             as_f32(part[h * d:(h + 1) * d, t, :])).then_inc(q_in[s], DMA)
                        if t == 1:
                            nb = (b + 1) % B
                            src = (x_in if L == 1 else x_out)[nb].rearrange("(k p) s -> p k s", p=P)
                            sp.wait_ge(x_split, it + 1)
                            for i in range(2):
                                sp.wait_ge(stored[i], 1 + it * (2 * DMA))
                            sp.dma_start(x_raw[:, :, :], src).then_inc(x_in_s, DMA)
                    sp.wait_ge(pv, 1 + (it + 1) * (T * KT))
                    sp.dma_start(x_res, (x_in if L == 1 else x_out)[b].rearrange("(k p) s -> p k s", p=P))\
                        .then_inc(res_in, DMA)
                    for o in range(CK):
                        sp.wait_ge(added, 1 + it * CK + o + 1)
                        sp.dma_start(x_out[b][o * P:(o + 1) * P, :], stage[:, o % 2, :]).then_inc(stored[o % 2], DMA)
            for i in range(2):
                sp.wait_ge(stored[i], 1 + L * B * CK // 2 * DMA)

        @block.gpsimd
        def _(pool):
            for credit in (scored, pv, shifted, added, q_proj, q_taken, *stored):
                pool.sem_inc(credit, 1)
            pool.memset(ident[:, :], 0.0).then_inc(consts, 1)
            pool.wait_ge(consts, 1)
            pool.affine_select(out=ident[:, :], in_=ident[:, :], compare_op=ALU.not_equal, fill=1.0, base=0,
                               pattern=[[-1, P]], channel_multiplier=1).then_inc(consts, 1)
            if not has_norm:
                pool.iota(key_no_i, pattern=[[1, S]], base=0, channel_multiplier=0).then_inc(consts, 1)

            def split_x(n):
                pool.wait_ge(x_hi_done, n + 1)
                for k in range(CK):
                    last = pool.tensor_tensor(x_lo[:, k, :], x_raw[:, k, :], as_f32(x_hi[:, k, :]), ALU.subtract)
                if not has_norm:
                    last.then_inc(x_split, 1)
                    return
                pool.wait_ge(ssum_done, n)
                first = n * SQ
                pool.tensor_tensor(sq[:, 0, :], x_raw[:, 0, :], x_raw[:, 0, :], ALU.mult).then_inc(sq_step, 1)
                for k in range(1, CK):
                    ins = pool.tensor_tensor(sq[:, 1, :], x_raw[:, k, :], x_raw[:, k, :], ALU.mult)
                    ins.then_inc(sq_step, 1)
                    if k == CK - 1:
                        pool.wait_ge(sq_step, first + 2 * k)
                        pool.tensor_tensor(sq[:, 0, :], sq[:, 0, :], sq[:, 1, :], ALU.add).then_inc(x_split, 1)
                    else:
                        pool.wait_ge(sq_step, first + 2 * k)
                        pool.tensor_tensor(sq[:, 0, :], sq[:, 0, :], sq[:, 1, :], ALU.add).then_inc(sq_step, 1)
                        pool.wait_ge(sq_step, first + 2 * k + 1)

            SQ = 2 * CK - 2
            split_x(0)
            with layers(pool) as l:
                with pool.Fori(0, B) as b:
                    it = b if L == 1 else l * B + b
                    for t in range(T):
                        pool.wait_ge(q_hi, it * T + t + 1)
                        pool.tensor_tensor(a_lo[:, t, :], stage[:, t % 2, :], as_f32(a_hi[:, t, :]), ALU.subtract)\
                            .then_inc(q_lo, 1)
                    split_x(it + 1)
                    for t in range(T):
                        pool.wait_ge(o_hi, it * T + t + 1)
                        pool.tensor_tensor(a_lo[:, t, :], stage[:, t % 2, :], as_f32(a_hi[:, t, :]), ALU.subtract)\
                            .then_inc(o_lo, 1)

        @block.scalar
        def _(act):
            def inv_rms(n):
                act.wait_ge(ms_step, 2 * (n + 1))
                act.wait_ge(q_taken, 1 + n * T)
                act.activation(inv[:, :], ms[:, 1, :], ACT.Sqrt, scale=scale * scale).then_inc(inv_done, 1)

            def round_x(n):
                act.wait_ge(x_in_s, (n + 1) * DMA)
                act.wait_ge(q_proj, 1 + n * T)
                act.activation(x_hi[:, :, :], x_raw[:, :, :], ACT.Copy).then_inc(x_hi_done, 1)

            round_x(0)
            if has_norm:
                inv_rms(0)
            with layers(act) as l:
                for c in range(WCH):
                    act.wait_ge(w_in[c % 2], (l * (WCH // 2) + c // 2 + 1) * DMA)
                    half = WCH // 2
                    n = (CK if c < half else T) // half
                    raw = w_raw[:, c % 2, :].rearrange("p (k n) -> p k n", k=n)
                    for i in range(n):
                        k = (c % half) * n + i
                        if c < half and has_norm:
                            act.wait_ge(nw_in, (l + 1) * DMA)
                            ins = act.activation(wq_hi[:, k, :], raw[:, i, :], ACT.Copy, scale=nw[:, k:k + 1])
                        else:
                            ins = act.activation((wq_hi if c < half else wo_hi)[:, k, :], raw[:, i, :], ACT.Copy)
                    ins.then_inc(w_rounded, 1)
                with act.Fori(0, B) as b:
                    it = b if L == 1 else l * B + b

                    def shift(t):
                        act.wait_ge(turned, it * T + t + 1)
                        for h in range(H):
                            ins = act.activation(q_ops[SHIFT:SHIFT + 1, t % RING, h, PASS - 1, :],
                                                 ps[32 * h:32 * h + 1, MAXB[1], :], ACT.Copy)
                        ins.then_inc(shifted, 1)

                    for t in range(T):
                        act.wait_ge(q_taken, 1 + it * T + t + 1)
                        act.activation(a_hi[:, t, :], stage[:, t % 2, :], ACT.Copy).then_inc(q_hi, 1)
                    def round_output(t):
                        act.wait_ge(normed, it * T + t + 1)
                        act.activation(a_hi[:, t, :], stage[:, t % 2, :], ACT.Copy).then_inc(o_hi, 1)

                    shift(0)
                    for t in range(T):
                        for s in range(NS):
                            if t > 0 and s == NS // 2:
                                round_output(t - 1)
                            act.wait_ge(scored, 1 + (it * T + t) * NS + s + 1)
                            if t > 0:
                                act.wait_ge(pv, 1 + (it * T + t - 1) * KT + s * KT // NS + 1)
                            act.activation(probs[:, s % kind.PS], ps[:, 2 * (s % 2):2 * (s % 2) + 2, :], ACT.Exp)\
                                .then_inc(exped, 1)
                        if t + 1 < T:
                            shift(t + 1)
                        if t == 0:
                            round_x(it + 1)
                    round_output(T - 1)
                    if has_norm:
                        inv_rms(it + 1)

        @block.vector
        def _(dve):
            dve.memset(max_cols[:, :, :], 0.0).then_inc(consts_v, 1)
            dve.memset(ones[:, :], 1.0).then_inc(consts_v, 1)
            dve.memset(as_f32(q_ops[X0:P, :, :, PASS - 1, :]), 0.0).then_inc(consts_v, 1)
            dve.memset(as_f32(k_ops[X0:P, :, :, PASS - 1, :]), 0.0).then_inc(consts_v, 1)
            dve.wait_ge(consts_v, 4)
            dve.memset(as_f32(k_ops[SHIFT:SHIFT + 1, :, :, PASS - 1, :]), 1.0).then_inc(consts_v, 1)
            if not has_norm:
                dve.wait_ge(rows_in, 5 * DMA)
                dve.wait_ge(consts, 3)
                step = [0]

                def then(ins):
                    step[0] += 1
                    ins.then_inc(brow_step, 1)
                    dve.wait_ge(brow_step, step[0])

                then(dve.tensor_scalar(brow, mrow, -1.0, 1.0, ALU.mult, ALU.add))
                then(dve.tensor_scalar(mrow, brow, -SUPPRESS, None, ALU.mult))
                dve.tensor_copy(b_hi, mrow).then_inc(bias_rows, 1)
                dve.wait_ge(bias_rows, 1)
                dve.tensor_tensor(b_lo, mrow, as_f32(b_hi), ALU.subtract).then_inc(bias_rows, 1)
                then(dve.tensor_copy(tok[:, :], tok_i[:, :]))
                then(dve.tensor_scalar(tok_w[:, :], tok[:, :], 0.0, float(S), ALU.is_lt, ALU.mult))
                then(dve.tensor_tensor(tok[:, :], tok[:, :], tok_w[:, :], ALU.add))
                then(dve.tensor_copy(key_no, key_no_i))
                for i in range(4):
                    then(dve.tensor_scalar(hit[:, i, :], key_no, tok[:, i:i + 1], None, ALU.is_equal))
                then(dve.tensor_tensor(hit[:, 0, :], hit[:, 0, :], hit[:, 1, :], ALU.max))
                then(dve.tensor_tensor(hit[:, 2, :], hit[:, 2, :], hit[:, 3, :], ALU.max))
                then(dve.tensor_scalar(hit[:, 1, :], hit[:, 2, :], -1.0, 1.0, ALU.mult, ALU.add))
                dve.tensor_tensor(ind[0], hit[:, 0, :], hit[:, 1, :], ALU.mult).then_inc(bias_rows, 2)
                dve.tensor_copy(ind[1], hit[:, 2, :]).then_inc(bias_rows, 2)

            def mean_square(n):
                dve.wait_ge(ssum_done, n + 1)
                dve.wait_ge(inv_done, n)
                dve.tensor_scalar(ms[:, 0, :], bank(5), 1.0 / C, EPS, ALU.mult, ALU.add).then_inc(ms_step, 1)
                dve.wait_ge(ms_step, 2 * n + 1)
                dve.reciprocal(ms[:, 1, :], ms[:, 0, :]).then_inc(ms_step, 1)

            if has_norm:
                mean_square(0)
            with layers(dve) as l:
                for c in range(WCH):
                    dve.wait_ge(w_rounded, l * WCH + c + 1)
                    half = WCH // 2
                    n = (CK if c < half else T) // half
                    raw = w_raw[:, c % 2, :].rearrange("p (k n) -> p k n", k=n)
                    for i in range(n):
                        k = (c % half) * n + i
                        hi, lo = (wq_hi, wq_lo) if c < half else (wo_hi, wo_lo)
                        if c < half and has_norm:
                            ins = dve.scalar_tensor_tensor(out=lo[:, k, :], in0=raw[:, i, :], scalar=nw[:, k:k + 1],
                                                           in1=as_f32(hi[:, k, :]), op0=ALU.mult, op1=ALU.subtract)
                        else:
                            ins = dve.tensor_tensor(lo[:, k, :], raw[:, i, :], as_f32(hi[:, k, :]), ALU.subtract)
                    ins.then_inc(w_split, 1)
                with dve.Fori(0, B) as b:
                    it = b if L == 1 else l * B + b

                    def reduce_max(t):
                        for n in range(M):
                            dve.wait_ge(smax, (it * T + t) * M + n + 1)
                            dve.tensor_reduce(max_cols[:, n % QT, 32 * (n // QT):32 * (n // QT) + 1],
                                              bank(MAXB[n % 2]), AX.X, ALU.max, negate=True).then_inc(reduced, 1)

                    for t in range(T):
                        dve.wait_ge(q_proj, 1 + it * T + t + 1)
                        if t < 2:
                            dve.wait_ge(stored[t], 1 + it * (2 * DMA))
                        else:
                            dve.wait_ge(q_lo, it * T + t - 1)
                        if has_norm:
                            dve.wait_ge(inv_done, it + 1)
                            ins = dve.tensor_tensor(stage[:, t % 2, :], bank(Q_BANK[t % 4]), inv[:, :], ALU.mult)
                        else:
                            ins = dve.tensor_scalar(stage[:, t % 2, :], bank(Q_BANK[t % 4]), scale, None, ALU.mult)
                        ins.then_inc(q_taken, 1)
                    reduce_max(0)
                    for t in range(T):
                        if t + 1 < T:
                            reduce_max(t + 1)
                        dve.wait_ge(pv, 1 + (it * T + t + 1) * KT)
                        dve.reciprocal(recip[:, :], bank(DENB)).then_inc(recip_done, 1)
                        dve.wait_ge(recip_done, it * T + t + 1)
                        if t < 2:
                            dve.wait_ge(q_lo, (it + 1) * T)
                        else:
                            dve.wait_ge(o_lo, it * T + t - 1)
                        dve.tensor_tensor(stage[:, t % 2, :], bank(OUTB), recip[:, :], ALU.mult).then_inc(normed, 1)
                    if has_norm:
                        mean_square(it + 1)
                    dve.wait_ge(res_in, (it + 1) * DMA)
                    for o in range(CK):
                        dve.wait_ge(o_proj, it * CK + o + 1)
                        if o >= 2:
                            dve.wait_ge(stored[o % 2], 1 + it * (2 * DMA) + DMA)
                        if has_norm:
                            ins = dve.tensor_tensor(stage[:, o % 2, :], bank(o), x_res[:, o, :], ALU.add)
                        else:
                            ins = dve.scalar_tensor_tensor(out=stage[:, o % 2, :], in0=bank(o),
                                                           scalar=bo_cols[:, o:o + 1], in1=x_res[:, o, :],
                                                           op0=ALU.add, op1=ALU.add)
                        ins.then_inc(added, 1)

        @block.tensor
        def _(pe):
            def sum_squares(n):
                pe.wait_ge(x_split, n + 1)
                pe.matmul(bank(5), ones[:, :], sq[:, 0, :], start=True, stop=True).then_inc(ssum_done, 1)

            pe.wait_ge(consts, 2)
            pe.wait_ge(consts_v, 5)
            if has_norm:
                sum_squares(0)
            else:
                pe.wait_ge(rows_set, 6 * H * RING * DMA)
            with layers(pe) as l:
                with pe.Fori(0, B) as b:
                    it = b if L == 1 else l * B + b
                    pe.wait_ge(w_split, (l + 1) * WCH)
                    if has_norm:
                        pe.wait_ge(ms_step, 2 * (it + 1))
                    pe.wait_ge(x_split, it + 1)
                    pe.wait_ge(shifted, 1 + it * T)
                    for t in range(T):
                        if t >= 4:
                            pe.wait_ge(q_taken, 1 + it * T + t - 3)
                        for k in range(CK):
                            for i, (w, x) in enumerate(((wq_hi, x_hi), (wq_hi, x_lo), (wq_lo, x_hi))):
                                last = pe.matmul(bank(Q_BANK[t % 4]), w[:, k, t * P:(t + 1) * P], x[:, k, :],
                                                 start=(k == 0 and i == 0), stop=(k == CK - 1 and i == 2))
                        last.then_inc(q_proj, 1)

                    def maxima(t, n):
                        s = t % RING
                        if n == 0:
                            pe.wait_ge(k_in[s], (it * uses[s] + t // RING + 1) * (3 * DMA))
                            pe.wait_ge(q_in[s], (it * uses[s] + t // RING + 1) * (3 * H * DMA))
                        elif n == 1:
                            pe.wait_ge(shifted, 1 + it * T + t)
                        else:
                            pe.wait_ge(reduced, (it * T + t) * M + n - 1)
                        h, q = n // QT, n % QT
                        for p in range(PASS):
                            last = pe.matmul(bank(MAXB[n % 2]), q_ops[0:rows(p), s, h, p, q * P:(q + 1) * P],
                                             k_ops[0:rows(p), s, k_head(h), p, :], start=(p == 0), stop=(p == PASS - 1))
                        last.then_inc(smax, 1)

                    def turn(t):
                        pe.wait_ge(reduced, (it * T + t + 1) * M)
                        for q in range(QT):
                            last = pe.transpose(ps[:, MAXB[1], q * P:(q + 1) * P], max_cols[:, q, :], ident[:, :])
                        last.then_inc(turned, 1)

                    def scores(t, n):
                        s, kt, hp = t % RING, n // (H // 2), n % (H // 2)
                        if n == 0:
                            pe.wait_ge(shifted, 1 + it * T + t + 1)
                        if t > 0 or n >= 2:
                            pe.wait_ge(exped, (it * T + t) * NS + n - 1)
                        for j in range(2):
                            h = 2 * hp + j
                            for p in range(PASS):
                                last = pe.matmul(bank(2 * (n % 2) + j), k_ops[:, s, k_head(h), p, kt * P:(kt + 1) * P],
                                                 q_ops[:, s, h, p, :], start=(p == 0), stop=(p == PASS - 1))
                        last.then_inc(scored, 1)

                    def outputs(t, kt):
                        if kt == 0:
                            if kind.shared:
                                if t == 0:
                                    pe.wait_ge(v_in[0], (it + 1) * DMA)
                            else:
                                pe.wait_ge(v_in[t % VR], (it * (T // VR) + t // VR + 1) * DMA)
                            if t > 0:
                                pe.wait_ge(normed, it * T + t)
                        pe.wait_ge(exped, (it * T + t) * NS + (kt + 1) * (H // 2))
                        for part in range(2):
                            for h in range(H):
                                rhs = probs[:, (kt * (H // 2) + h // 2) % kind.PS, h % 2, :]
                                c0 = (t if kind.shared else h) * d
                                lhs = v[:, 0 if kind.shared else t % VR, kt, c0:c0 + d] if part == 0 else ones[:, 0:d]
                                last = pe.matmul(ps[h * d:(h + 1) * d, OUTB if part == 0 else DENB, :], lhs, rhs,
                                                 start=(kt == 0), stop=(kt == KT - 1), skip_group_check=True)
                        last.then_inc(pv, 1)

                    def project_out(t):
                        pe.wait_ge(o_lo, it * T + t + 1)
                        for o in range(CK):
                            for i, (w, a) in enumerate(((wo_hi, a_hi), (wo_hi, a_lo), (wo_lo, a_hi))):
                                last = pe.matmul(bank(o), w[:, t, o * P:(o + 1) * P], a[:, t, :],
                                                 start=(t == 0 and i == 0), stop=(t == T - 1 and i == 2))
                            if t == T - 1:
                                last.then_inc(o_proj, 1)

                    pe.wait_ge(q_taken, 1 + (it + 1) * T)
                    for n in range(M):
                        maxima(0, n)
                    turn(0)
                    pe.wait_ge(added, 1 + it * CK)
                    for t in range(T):
                        for kt in range(KT):
                            for n in range(kt * (H // 2), (kt + 1) * (H // 2)):
                                scores(t, n)
                                if t + 1 < T:
                                    maxima(t + 1, 2 * n)
                                    maxima(t + 1, 2 * n + 1)
                            if kt > 0:
                                outputs(t, kt - 1)
                        if t + 1 < T:
                            turn(t + 1)
                        outputs(t, KT - 1)
                    pe.wait_ge(exped, (it + 1) * (T * NS))
                    if has_norm:
                        sum_squares(it + 1)
                    for t in range(T):
                        project_out(t)


def build(nc, a, out):
    k_scratch = nc.dram_tensor("k_scratch", (B, PROJ // P, 2, P, S), F32, kind="Internal").ap()
    v_scratch = nc.dram_tensor("v_scratch", (B, KT, P, PROJ), F32, kind="Internal").ap()
    project_context(nc, "kp", a["ctx_t"], a["wk"], k_scratch, True)
    project_context(nc, "vp", a["ctx_t"], a["wv"], v_scratch, False)
    bias = dict(bo=a["bo"], mask_a=a["mask_a"], mask_b=a["mask_b"], tok_a=a["tok_a"], tok_b=a["tok_b"])
    attention_layers(nc, "a0", Kind(1, INNER0, 64, False, 4), a["x_t"], out, k_scratch, v_scratch,
                     a["wq0"], a["wo0"], bias=bias)
    attention_layers(nc, "a1", Kind(LAYERS, INNER, 32, True, 8), out, out, k_scratch, v_scratch,
                     a["wq"], a["wo"], norm_w=a["norm_w"])


def kernel(**inputs):
    import numpy as np
    import concourse.bacc as bacc
    from concourse.bass_utils import run_bass_kernel_spmd

    own = range(1, LAYERS + 1)
    arrays = {
        "x_t": inputs["x"].transpose(0, 2, 1),
        "ctx_t": inputs["ctx_2048"].transpose(0, 2, 1),
        "wk": np.concatenate([inputs["L0_xattn_Wk"]] + [inputs[f"L{i}_xattn_wk"] for i in own], axis=1),
        "wv": np.concatenate([inputs["L0_xattn_Wv"]] + [inputs[f"L{i}_xattn_wv"] for i in own], axis=1),
        "wq0": inputs["L0_xattn_Wq"][None],
        "wo0": inputs["L0_xattn_Wo"][None],
        "wq": np.stack([inputs[f"L{i}_xattn_wq"] for i in own]),
        "wo": np.stack([inputs[f"L{i}_xattn_wo"] for i in own]),
        "norm_w": np.stack([inputs[f"L{i}_xattn_norm_w"].reshape(CK, P).T for i in own]),
        "bo": inputs["L0_xattn_bo"].reshape(CK, P).T,
        "mask_a": inputs["mask_S_fk1"],
        "mask_b": inputs["mask_S_fk0"],
        "tok_a": inputs["L0_xattn_token_indices_A"],
        "tok_b": inputs["L0_xattn_token_indices_B"],
    }
    arrays = {n: np.ascontiguousarray(x) for n, x in arrays.items()}
    nc = bacc.Bacc("TRN2", target_bir_lowering=False, num_devices=1)
    aps = {n: nc.dram_tensor(f"in_{n}", x.shape, mybir.dt.from_np(x.dtype), kind="ExternalInput").ap()
           for n, x in arrays.items()}
    out = nc.dram_tensor("out_t", (B, C, S), F32, kind="ExternalOutput").ap()
    build(nc, aps, out)
    r = run_bass_kernel_spmd(nc, [{f"in_{n}": x for n, x in arrays.items()}], core_ids=[0])
    return np.ascontiguousarray(r.results[0]["out_t"].transpose(0, 2, 1))
```

```python
from contextlib import ExitStack

import concourse.bass as bass
from concourse import mybir

P = 128
W = 512
F32 = mybir.dt.float32
F32R = mybir.dt.float32r
I32 = mybir.dt.int32
ALU = mybir.AluOpType
ACT = mybir.ActivationFunctionType
AX = mybir.AxisListType

B = 8
C = 512
CT = 1024
S = 512
INNER0 = 1024
INNER = 512
KV = 128
LAYERS = 3
PROJ = INNER0 + LAYERS * KV
KT = S // P
QT = S // P
CK = C // P
EPS = 1e-5
SUPPRESS = 20.0
DMA = 16
SHIFT = 96
BIAS = 64



def as_f32(ap):
    return ap.bitcast(F32)


def project_context(nc, name, ctx_t, weights, scratch, is_k):
    KC = CT // P
    VP = 3
    WB = PROJ // P if is_k else KT * VP
    NCH = KC // 2
    CHUNK_AT = {2 * j + 1: j for j in range(NCH)}
    with ExitStack() as mem:
        def sb(n, shape, dt):
            return mem.enter_context(nc.sbuf_tensor(f"{name}_{n}", shape, dt))

        def sem(n):
            return mem.enter_context(nc.semaphore(f"{name}_{n}"))

        w_hi = sb("w_hi", [P, KC, PROJ], F32R)
        w_lo = sb("w_lo", [P, KC, PROJ], F32R)
        c_hi = [sb(f"c_hi{i}", [P, KC, S], F32R) for i in range(2)]
        c_lo = [sb(f"c_lo{i}", [P, KC, S], F32R) for i in range(2)]
        raw = sb("raw", [P, 2, PROJ], F32)
        out = [sb(f"out{i}", [P, 2, W], F32R) if is_k else sb(f"out{i}", [P, 1, W], F32) for i in range(2)]
        ps = mem.enter_context(nc.psum_tensor(f"{name}_ps", [P, 2, W], F32))

        raw_in = [sem(f"raw_in{i}") for i in range(2)]
        hi_done = sem("hi_done")
        lo_done = sem("lo_done")
        block_done = sem("block_done")
        out_hi = sem("out_hi")
        out_lo = sem("out_lo")
        stored = [sem(f"stored{i}") for i in range(2)]

        w_rows = weights.rearrange("(k p) n -> p k n", p=P)
        taken = out_lo if is_k else out_hi

        def chunk_view(j):
            return raw[:, j % 2, 0:2 * S].rearrange("p (k s) -> p k s", k=2)

        def width(n):
            return W if is_k or n % VP < 2 else LAYERS * KV

        def raw_count(b, j):
            return b * (DMA * NCH // 2) + DMA * (KC // 2 + j // 2 + 1)

        block = mem.enter_context(nc.Block())

        @block.gpsimd
        def _(pool):
            for credit in (taken, *stored):
                pool.sem_inc(credit, 1)

        @block.sync
        def _(sp):
            def load(b, place, j):
                sp.wait_ge(lo_done, place * NCH + KC + j - 1)
                src = ctx_t[b].rearrange("(k p) s -> p k s", p=P)
                sp.dma_start(chunk_view(j), src[:, 2 * j:2 * j + 2, :]).then_inc(raw_in[j % 2], DMA)

            for k in range(KC):
                if k >= 2:
                    sp.wait_ge(lo_done, k - 1)
                sp.dma_start(raw[:, k % 2, :], w_rows[:, k, :]).then_inc(raw_in[k % 2], DMA)
            for j in range(NCH):
                load(0, 0, j)
            with sp.Fori(0, B // 2) as bb:
                for par in range(2):
                    b = bb * 2 + par
                    for n in range(WB):
                        m = par * WB + n
                        sp.wait_ge(taken, 1 + b * WB + n + 1)
                        if is_k:
                            dst = scratch[b, n].rearrange("c p s -> p c s")
                        else:
                            dst = scratch[b, n // VP][:, (n % VP) * W:(n % VP) * W + width(n)]\
                                .rearrange("p (c s) -> p c s", c=1)
                        src = out[m % 2][:, :, 0:width(n)]
                        sp.dma_start(dst, as_f32(src) if is_k else src).then_inc(stored[m % 2], DMA)
                        if n in CHUNK_AT:
                            load((b + 1) % B, b + 1, CHUNK_AT[n])
            for i in range(2):
                sp.wait_ge(stored[i], 1 + DMA * WB * B // 2)

        @block.scalar
        def _(act):
            def round_chunk(place, par, j):
                act.wait_ge(raw_in[j % 2], raw_count(place, j))
                act.activation(c_hi[par][:, 2 * j:2 * j + 2, :], chunk_view(j), ACT.Copy).then_inc(hi_done, 1)

            for k in range(KC):
                act.wait_ge(raw_in[k % 2], DMA * (k // 2 + 1))
                act.activation(w_hi[:, k, :], raw[:, k % 2, :], ACT.Copy).then_inc(hi_done, 1)
            for j in range(NCH):
                round_chunk(0, 0, j)
            with act.Fori(0, B // 2) as bb:
                for par in range(2):
                    b = bb * 2 + par
                    for n in range(WB):
                        m = par * WB + n
                        w = width(n)
                        act.wait_ge(block_done, b * WB + n + 1)
                        act.wait_ge(stored[m % 2], 1 + bb * (DMA * WB) + DMA * (m // 2))
                        act.activation(out[m % 2][:, 0, 0:w], ps[:, m % 2, 0:w], ACT.Copy).then_inc(out_hi, 1)
                        if n in CHUNK_AT:
                            round_chunk(b + 1, 1 - par, CHUNK_AT[n])

        @block.vector
        def _(dve):
            def rest_chunk(place, par, j):
                dve.wait_ge(hi_done, place * NCH + KC + j + 1)
                dve.tensor_tensor(c_lo[par][:, 2 * j:2 * j + 2, :], chunk_view(j),
                                  as_f32(c_hi[par][:, 2 * j:2 * j + 2, :]), ALU.subtract).then_inc(lo_done, 1)

            for k in range(KC):
                dve.wait_ge(hi_done, k + 1)
                dve.tensor_tensor(w_lo[:, k, :], raw[:, k % 2, :], as_f32(w_hi[:, k, :]), ALU.subtract)\
                    .then_inc(lo_done, 1)
            for j in range(NCH):
                rest_chunk(0, 0, j)
            with dve.Fori(0, B // 2) as bb:
                for par in range(2):
                    b = bb * 2 + par
                    for n in range(WB):
                        m = par * WB + n
                        if is_k:
                            dve.wait_ge(out_hi, b * WB + n + 1)
                            dve.tensor_tensor(out[m % 2][:, 1, :], ps[:, m % 2, :], as_f32(out[m % 2][:, 0, :]),
                                              ALU.subtract).then_inc(out_lo, 1)
                        if n in CHUNK_AT:
                            rest_chunk(b + 1, 1 - par, CHUNK_AT[n])

        @block.tensor
        def _(pe):
            with pe.Fori(0, B // 2) as bb:
                for par in range(2):
                    b = bb * 2 + par
                    pe.wait_ge(lo_done, (b + 1) * NCH + KC)
                    for n in range(WB):
                        m = par * WB + n
                        if par == 0 and n < 2:
                            pe.wait_ge(taken, 1 + b * WB)
                        else:
                            pe.wait_ge(taken, 1 + b * WB + n - 1)
                        for k in range(KC):
                            if is_k:
                                pairs = [(w, c[par][:, k, :]) for w, c in ((w_hi, c_hi), (w_hi, c_lo), (w_lo, c_hi))]
                                pairs = [(w[:, k, n * P:(n + 1) * P], c) for w, c in pairs]
                            else:
                                t, c0 = n // VP, (n % VP) * W
                                pairs = [(c[par][:, k, t * P:(t + 1) * P], w[:, k, c0:c0 + width(n)])
                                         for c, w in ((c_hi, w_hi), (c_hi, w_lo), (c_lo, w_hi))]
                            for i, (stationary, moving) in enumerate(pairs):
                                last = pe.matmul(ps[:, m % 2, 0:width(n)], stationary, moving,
                                                 start=(k == 0 and i == 0), stop=(k == KC - 1 and i == 2))
                        last.then_inc(block_done, 1)


class Kind:

    def __init__(self, layers, inner, head, shared_kv):
        self.layers = layers
        self.d = head
        self.T = inner // P
        self.H = P // head
        self.shared = shared_kv
        self.PASS = 4 * head // P
        self.NS = self.H // 2 * KT
        self.M = self.H * QT
        self.KHEADS = 1 if shared_kv else self.H
        assert self.M == 2 * self.NS and self.T % RING == 0


RING = 4
AHEAD = 3


def attention_layers(nc, name, kind, x_in, x_out, k_scratch, v_scratch, wq, wo, norm_w=None, bias=None):
    L, d, T, H, NS, M, PASS = kind.layers, kind.d, kind.T, kind.H, kind.NS, kind.M, kind.PASS
    N = L * B
    has_norm = norm_w is not None
    scale = d ** -0.5
    UT = T // RING
    PV = 2 * KT
    SPLIT_AT = T - AHEAD
    RS = 4 if kind.shared else 1
    RES = 4 if kind.shared else 2
    UR = CK // RES
    XT = CK if has_norm else CK // 2
    XC = CK // XT
    SQ = 2 * CK - 1
    with ExitStack() as mem:
        def sb(n, shape, dt):
            return mem.enter_context(nc.sbuf_tensor(f"{name}_{n}", shape, dt))

        def sem(n):
            return mem.enter_context(nc.semaphore(f"{name}_{n}"))

        wq_hi = sb("wq_hi", [P, CK, T * P], F32R)
        wq_lo = sb("wq_lo", [P, CK, T * P], F32R)
        wo_hi = sb("wo_hi", [P, T, C], F32R)
        wo_lo = sb("wo_lo", [P, T, C], F32R)
        x_hi = sb("x_hi", [P, CK, S], F32R)
        x_lo = sb("x_lo", [P, CK, S], F32R)
        x_raw = sb("x_raw", [P, XT, S], F32)
        x_res = sb("x_res", [P, RS, S], F32) if has_norm else x_raw[:, 1:2, :]
        qn_hi = sb("qn_hi", [P, S], F32R)
        qn_lo = sb("qn_lo", [P, S], F32R)
        a_hi = sb("a_hi", [P, T, S], F32R)
        a_lo = sb("a_lo", [P, T, S], F32R)
        q_ops = sb("q_ops", [P, RING, H, PASS, S], F32R)
        k_ops = sb("k_ops", [P, RING, kind.KHEADS, PASS, S], F32R)
        v = sb("v", [P, KT, P], F32)
        probs = sb("probs", [P, NS, 2, S], F32)
        stage = sb("stage", [P, 2, S], F32)
        results = sb("results", [P, RES, S], F32) if has_norm else stage
        max_cols = sb("max_cols", [P, P + QT], F32)
        ident = sb("ident", [P, P], F32)
        ones = sb("ones", [P, P if has_norm else d], F32)
        if has_norm:
            w_raw = sb("w_raw", [P, 1, 4 * W], F32)
            qf = sb("qf", [P, S], F32)
            inv = sb("inv", [P, S], F32)
            sq = sb("sq", [P, 2, S], F32)
            ms = sb("ms", [P, 2, S], F32)
            nw = sb("nw", [P, CK], F32)
        else:
            w_raw = probs[:, 0:4].rearrange("p (a b) c s -> p a (b c s)", a=2)
            bo_cols = sb("bo_cols", [P, C // P], F32)
            spare = probs[:, 0:4].rearrange("p a c s -> p (a c) s")
            hit = spare[0:1, 0:4, :]
            mrow, brow = spare[0:2, 4, :], spare[0:2, 5, :]
            key_no, key_no_i = spare[0:1, 6, :], spare[0:1, 7, :].bitcast(I32)
            b_hi, b_lo = brow.bitcast(F32R), stage[0:2, 0, :].bitcast(F32R)
            ind = [stage[0:1, 1, :].bitcast(F32R), hit[:, 3, :].bitcast(F32R)]
            tok_i = v[0:1, 0, 0:4].bitcast(I32)
            tok, tok_w = v[0:1, 0, 4:8], v[0:1, 0, 8:12]
        ps = mem.enter_context(nc.psum_tensor(f"{name}_ps", [P, 8, W], F32))
        MAXB, OUTB, DENB = (4, 5), 6, 7
        TURNB, QB, SUMB = 4, 5, 5
        OB = (4, 5, 2, 3)

        consts = sem("consts")
        consts_v = sem("consts_v")
        rows_in = sem("rows_in")
        brow_step = sem("brow_step")
        bias_rows = sem("bias_rows")
        rows_set = sem("rows_set")
        w_in = [sem(f"w_in{i}") for i in range(2)]
        nw_in = sem("nw_in")
        w_rounded = sem("w_rounded")
        w_split = sem("w_split")
        x_in_s = sem("x_in")
        x_hi_done = sem("x_hi_done")
        x_split = sem("x_split")
        sq_step = sem("sq_step")
        ssum_done = sem("ssum_done")
        ms_step = sem("ms_step")
        inv_done = sem("inv_done")
        q_proj = sem("q_proj")
        q_taken = sem("q_taken")
        q_hi = sem("q_hi")
        q_lo = sem("q_lo")
        q_in = [sem(f"q_in{i}") for i in range(RING)]
        k_in = [sem(f"k_in{i}") for i in range(RING)]
        v_in = sem("v_in")
        smax = sem("smax")
        reduced = sem("reduced")
        turned = sem("turned")
        shifted = sem("shifted")
        scored = sem("scored")
        exped = sem("exped")
        pv = sem("pv")
        recip_done = sem("recip_done")
        normed = sem("normed")
        o_hi = sem("o_hi")
        o_lo = sem("o_lo")
        o_proj = sem("o_proj")
        res_in = [sem(f"res_in{i}") for i in range(RS)]
        added = sem("added")
        stored = [sem(f"stored{i}") for i in range(RES)]

        def bank(i):
            return ps[:, i, :]

        def k_head(h):
            return 0 if kind.shared else h

        def rows(p):
            return SHIFT if p == PASS - 1 else P

        def place(it, t):
            return (it + 1, t - T) if t >= T else (it, t)

        def ring_count(it, t):
            return it * UT + t // RING + 1

        WCH = 2 * T * P * CK // (4 * W)
        HALF = WCH // 2

        def chunk(w, c):
            src = w.rearrange("(k p) n -> p k n", p=P)
            n = src.shape[1] // HALF
            return src[:, (c % HALF) * n:(c % HALF + 1) * n, :]

        def raw_chunk(c, slot):
            n = (CK if c < HALF else T) // HALF
            return w_raw[:, slot, :].rearrange("p (k n) -> p k n", k=n), range((c % HALF) * n, (c % HALF + 1) * n)

        block = mem.enter_context(nc.Block())
        X0 = P - d

        @block.sync
        def _(sp):
            def load_k(it, t, n=None):
                s = t % RING
                b, l = (0, 0) if n is None else (n % B, n // B)
                for i, part in enumerate((0, 1, 0)):
                    at = (i * d) % P
                    dst = as_f32(k_ops[at:at + d, s, :, (i * d) // P, :])
                    if kind.shared:
                        src = k_scratch[b, INNER0 // P + l, part][t * d:(t + 1) * d, :]
                        src = src.rearrange("(h p) s -> p h s", h=1)
                    else:
                        src = k_scratch[b, t, part].rearrange("(h p) s -> p h s", h=H)
                    sp.dma_start(dst, src).then_inc(k_in[s], DMA)

            def load_q(it, t):
                s = t % RING
                sp.wait_ge(q_lo, it * T + t + 1)
                for h in range(H):
                    for i, part in enumerate((qn_hi, qn_hi, qn_lo)):
                        at = (i * d) % P
                        sp.dma_start(as_f32(q_ops[at:at + d, s, h, (i * d) // P, :]),
                                     as_f32(part[h * d:(h + 1) * d, :])).then_inc(q_in[s], DMA)

            def load_v(t, n=None):
                b, l = (0, 0) if n is None else (n % B, n // B)
                src = v_scratch[b].rearrange("k p n -> p k n")
                if kind.shared:
                    sp.dma_start(v[:, :, :], src[:, :, bass.ds(INNER0 + l * KV, KV)]).then_inc(v_in, DMA)
                else:
                    sp.dma_start(v[:, :, :], src[:, :, t * P:(t + 1) * P]).then_inc(v_in, DMA)

            def load_x(b, c):
                src = x_in[b].rearrange("(k p) s -> p k s", p=P)[:, c * XT:(c + 1) * XT, :]
                sp.dma_start(x_raw[:, :, :], src).then_inc(x_in_s, DMA)

            load_x(0, 0)
            if has_norm:
                sp.dma_start(nw[:, :], norm_w[0]).then_inc(nw_in, DMA)
                sp.dma_start(w_raw[:, 0, :].rearrange("p (k n) -> p k n", k=CK), chunk(wq[0], 0)).then_inc(w_in[0], DMA)
            else:
                sp.dma_start(bo_cols[:, :], bias["bo"]).then_inc(rows_in, DMA)
                for i, m in enumerate(("mask_a", "mask_b")):
                    sp.dma_start(spare[i:i + 1, 4, :], bias[m].rearrange("(a s) -> a s", a=1)).then_inc(rows_in, DMA)
                for i, m in enumerate(("tok_a", "tok_b")):
                    sp.dma_start(tok_i[:, 2 * i:2 * i + 2], bias[m].rearrange("(a s) -> a s", a=1))\
                        .then_inc(rows_in, DMA)
                sp.wait_ge(bias_rows, 6)
                sp.wait_ge(consts_v, 4)
                for s in range(RING):
                    for h in range(H):
                        q_row = as_f32(q_ops[:, s, h, PASS - 1, :])
                        k_row = as_f32(k_ops[:, s, h, PASS - 1, :])
                        sp.dma_start(q_row[BIAS:BIAS + 2, :], as_f32(b_hi)).then_inc(rows_set, DMA)
                        sp.dma_start(q_row[BIAS + 2:BIAS + 4, :], as_f32(b_lo)).then_inc(rows_set, DMA)
                        for r in range(4):
                            sp.dma_start(k_row[BIAS + r:BIAS + r + 1, :], as_f32(ind[r % 2])).then_inc(rows_set, DMA)
                sp.wait_ge(rows_set, 6 * H * RING * DMA)
                for c in range(WCH):
                    if c >= 2:
                        sp.wait_ge(w_split, c - 1)
                    if 2 <= c <= XC:
                        sp.wait_ge(x_split, c - 1)
                        load_x(0, c - 1)
                    dst, ks = raw_chunk(c, c % 2)
                    sp.dma_start(dst, chunk((wq if c < HALF else wo)[0], c)).then_inc(w_in[c % 2], DMA)
            for t in range(AHEAD):
                load_k(0, t)
            load_v(0)
            for t in range(AHEAD):
                load_q(0, t)
            with sp.Fori(0, N) as it:
                nxt = (it + 1) % N
                for t in range(T):
                    sp.wait_ge(scored, 1 + (it * T + t) * NS)
                    it_q, t_q = place(it, t + AHEAD)
                    load_k(it_q, t_q, it if t + AHEAD < T else nxt)
                    if t == 0:
                        sp.wait_ge(x_split, (it + 1) * XC)
                        for i in range(RES):
                            sp.wait_ge(stored[i], 1 + it * (UR * DMA))
                        load_x(nxt % B, 0)
                        if has_norm:
                            with sp.If(it % B == 0):
                                dst = w_raw[:, 0, :].rearrange("p (k n) -> p k n", k=T)
                                sp.wait_ge(w_split, 2 * (it // B) + 1)
                                sp.dma_start(dst, chunk(wo[it // B], 1)).then_inc(w_in[0], DMA)
                            with sp.If(it % B == B - 1):
                                sp.wait_ge(w_split, 2 * (it // B) + 2)
                                sp.dma_start(w_raw[:, 0, :].rearrange("p (k n) -> p k n", k=CK),
                                             chunk(wq[nxt // B], 0)).then_inc(w_in[0], DMA)
                                sp.dma_start(nw[:, :], norm_w[nxt // B]).then_inc(nw_in, DMA)
                    if t == SPLIT_AT:
                        for c in range(1, XC):
                            sp.wait_ge(x_split, (it + 1) * XC + c)
                            load_x(nxt % B, c)
                    if t == T - 1:
                        src = x_in[it % B]
                        sp.wait_ge(added, 1 + it * CK)
                        if not has_norm:
                            sp.wait_ge(x_split, (it + 2) * XC)
                        for o in range(RS):
                            sp.dma_start(x_res[:, o, :], src[o * P:(o + 1) * P, :]).then_inc(res_in[o], DMA)
                    if not kind.shared:
                        sp.wait_ge(pv, 1 + (it * T + t + 1) * PV)
                        load_v((t + 1) % T, it if t + 1 < T else nxt)
                    if t < T - 1:
                        load_q(it_q, t_q)
                if kind.shared:
                    sp.wait_ge(pv, 1 + (it + 1) * (T * PV))
                    load_v(0, nxt)
                for o in range(CK):
                    sp.wait_ge(added, 1 + it * CK + o + 1)
                    sp.dma_start(x_out[it % B][o * P:(o + 1) * P, :], results[:, o % RES, :])                        .then_inc(stored[o % RES], DMA)
                    if o + RS < CK:
                        sp.dma_start(x_res[:, (o + RS) % RS, :],
                                     x_in[it % B][(o + RS) * P:(o + RS + 1) * P, :])\
                            .then_inc(res_in[(o + RS) % RS], DMA)
                load_q(it + 1, AHEAD - 1)
            for i in range(RES):
                sp.wait_ge(stored[i], 1 + N * UR * DMA)
            sp.wait_ge(x_in_s, (N + 1) * XC * DMA)
            for t in range(AHEAD):
                sp.wait_ge(k_in[t], ring_count(N, t) * (3 * DMA))
                sp.wait_ge(q_in[t], ring_count(N, t) * (3 * H * DMA))
            sp.wait_ge(v_in, (N + 1 if kind.shared else N * T + 1) * DMA)

        @block.gpsimd
        def _(pool):
            for credit in (scored, pv, added, normed, *stored):
                pool.sem_inc(credit, 1)
            pool.memset(ident[:, :], 0.0).then_inc(consts, 1)
            pool.wait_ge(consts, 1)
            pool.affine_select(out=ident[:, :], in_=ident[:, :], compare_op=ALU.not_equal, fill=1.0, base=0,
                               pattern=[[-1, P]], channel_multiplier=1).then_inc(consts, 1)
            if not has_norm:
                pool.iota(key_no_i, pattern=[[1, S]], base=0, channel_multiplier=0).then_inc(consts, 1)
            def split_x(n):
                for c in range(XC):
                    pool.wait_ge(x_hi_done, n * XC + c + 1)
                    for k in range(XT):
                        last = pool.tensor_tensor(x_lo[:, c * XT + k, :], x_raw[:, k, :],
                                                  as_f32(x_hi[:, c * XT + k, :]), ALU.subtract)
                    last.then_inc(x_split, 1)

            def squares(n):
                pool.wait_ge(x_in_s, (n + 1) * DMA)
                first = n * SQ
                pool.tensor_tensor(sq[:, 0, :], x_raw[:, 0, :], x_raw[:, 0, :], ALU.mult).then_inc(sq_step, 1)
                for k in range(1, CK):
                    pool.tensor_tensor(sq[:, 1, :], x_raw[:, k, :], x_raw[:, k, :], ALU.mult).then_inc(sq_step, 1)
                    pool.wait_ge(sq_step, first + 2 * k)
                    pool.tensor_tensor(sq[:, 0, :], sq[:, 0, :], sq[:, 1, :], ALU.add).then_inc(sq_step, 1)
                    if k < CK - 1:
                        pool.wait_ge(sq_step, first + 2 * k + 1)

            def rest_q(it, t):
                if has_norm:
                    pool.wait_ge(q_hi, it * T + t + 1)
                    pool.tensor_tensor(qn_lo[:, :], qf[:, :], as_f32(qn_hi[:, :]), ALU.subtract).then_inc(q_lo, 1)

            def rest_output(it, t):
                pool.wait_ge(o_hi, it * T + t + 1)
                pool.tensor_tensor(a_lo[:, t, :], stage[:, t % 2, :], as_f32(a_hi[:, t, :]), ALU.subtract)\
                    .then_inc(o_lo, 1)

            if has_norm:
                squares(0)
            split_x(0)
            for t in range(AHEAD):
                rest_q(0, t)
            with pool.Fori(0, N) as it:
                for t in range(T):
                    if t > 0:
                        rest_output(it, t - 1)
                    if t == SPLIT_AT:
                        split_x(it + 1)
                    if t == T - 1:
                        rest_output(it, t)
                    rest_q(*place(it, t + AHEAD))
                    if has_norm and t == SPLIT_AT - 1:
                        squares(it + 1)

        @block.scalar
        def _(act):
            def round_chunk(c, slot, count, l=0):
                act.wait_ge(w_in[slot], count * DMA)
                raw, ks = raw_chunk(c, slot)
                if c < HALF and has_norm:
                    act.wait_ge(nw_in, (l + 1) * DMA)
                for i, k in enumerate(ks):
                    if c < HALF and has_norm:
                        ins = act.activation(wq_hi[:, k, :], raw[:, i, :], ACT.Copy, scale=nw[:, k:k + 1])
                    else:
                        ins = act.activation((wq_hi if c < HALF else wo_hi)[:, k, :], raw[:, i, :], ACT.Copy)
                ins.then_inc(w_rounded, 1)

            def round_x(n, c):
                act.wait_ge(x_in_s, (n * XC + c + 1) * DMA)
                act.activation(x_hi[:, c * XT:(c + 1) * XT, :], x_raw[:, :, :], ACT.Copy).then_inc(x_hi_done, 1)

            def inv_rms(n):
                act.wait_ge(ms_step, 2 * (n + 1))
                act.activation(inv[:, :], ms[:, 1, :], ACT.Sqrt, scale=scale * scale).then_inc(inv_done, 1)

            def round_q(it, t, first=False):
                if has_norm:
                    act.wait_ge(q_taken, it * T + t + 1)
                else:
                    act.wait_ge(q_proj, it * T + t + 1)
                if not first:
                    it_p, t_p = (it, t - 1) if t > 0 else (it - 1, T - 1)
                    act.wait_ge(q_in[t_p % RING], ring_count(it_p, t_p) * (3 * H * DMA))
                if has_norm:
                    act.activation(qn_hi[:, :], qf[:, :], ACT.Copy).then_inc(q_hi, 1)
                else:
                    act.activation(qn_hi[:, :], bank(QB), ACT.Copy, scale=scale).then_inc(q_hi, 1)

            def shift(it, t):
                act.wait_ge(turned, it * T + t + 1)
                for h in range(H):
                    ins = act.activation(q_ops[SHIFT:SHIFT + 1, t % RING, h, PASS - 1, :],
                                         ps[32 * h:32 * h + 1, TURNB, :], ACT.Copy)
                ins.then_inc(shifted, 1)

            def round_output(it, t):
                act.wait_ge(normed, 1 + it * T + t + 1)
                act.activation(a_hi[:, t, :], stage[:, t % 2, :], ACT.Copy).then_inc(o_hi, 1)

            if has_norm:
                round_x(0, 0)
                round_chunk(0, 0, 1)
                inv_rms(0)
            else:
                for c in range(WCH):
                    round_chunk(c, c % 2, c // 2 + 1)
                    if c < XC:
                        round_x(0, c)
            for t in range(AHEAD):
                round_q(0, t, first=(t == 0))
            shift(0, 0)
            with act.Fori(0, N) as it:
                for t in range(T):
                    for s in range(NS):
                        act.wait_ge(scored, 1 + (it * T + t) * NS + s + 1)
                        act.activation(probs[:, s], ps[:, 2 * (s % 2):2 * (s % 2) + 2, :], ACT.Exp)\
                            .then_inc(exped, 1)
                        if t == SPLIT_AT and s % 2 == 1 and s // 2 < XC:
                            round_x(it + 1, s // 2)
                        if t > 0 and s == NS // 2:
                            round_output(it, t - 1)
                        if has_norm and t == 0 and s == NS // 2:
                            with act.If(it % B == 0):
                                round_chunk(1, 0, 2 * (it // B) + 2)
                        if has_norm and t == SPLIT_AT and s == NS // 2:
                            with act.If(it % B == B - 1):
                                round_chunk(0, 0, 2 * (it // B) + 3, it // B + 1)
                    shift(*place(it, t + 1))
                    if has_norm and t == SPLIT_AT:
                        inv_rms(it + 1)
                    round_q(*place(it, t + AHEAD))
                    if t == T - 1:
                        round_output(it, t)

        @block.vector
        def _(dve):
            dve.memset(max_cols[:, :], 0.0).then_inc(consts_v, 1)
            dve.memset(ones[:, :], 1.0).then_inc(consts_v, 1)
            dve.memset(as_f32(q_ops[X0:P, :, :, PASS - 1, :]), 0.0).then_inc(consts_v, 1)
            dve.memset(as_f32(k_ops[X0:P, :, :, PASS - 1, :]), 0.0).then_inc(consts_v, 1)
            dve.wait_ge(consts_v, 4)
            dve.memset(as_f32(k_ops[SHIFT:SHIFT + 1, :, :, PASS - 1, :]), 1.0).then_inc(consts_v, 1)
            if not has_norm:
                dve.wait_ge(rows_in, 5 * DMA)
                dve.wait_ge(consts, 3)
                step = [0]

                def then(ins):
                    step[0] += 1
                    ins.then_inc(brow_step, 1)
                    dve.wait_ge(brow_step, step[0])

                then(dve.tensor_scalar(brow, mrow, -1.0, 1.0, ALU.mult, ALU.add))
                then(dve.tensor_scalar(mrow, brow, -SUPPRESS, None, ALU.mult))
                dve.tensor_copy(b_hi, mrow).then_inc(bias_rows, 1)
                dve.wait_ge(bias_rows, 1)
                dve.tensor_tensor(b_lo, mrow, as_f32(b_hi), ALU.subtract).then_inc(bias_rows, 1)
                then(dve.tensor_copy(tok[:, :], tok_i[:, :]))
                then(dve.tensor_scalar(tok_w[:, :], tok[:, :], 0.0, float(S), ALU.is_lt, ALU.mult))
                then(dve.tensor_tensor(tok[:, :], tok[:, :], tok_w[:, :], ALU.add))
                then(dve.tensor_copy(key_no, key_no_i))
                for i in range(4):
                    then(dve.tensor_scalar(hit[:, i, :], key_no, tok[:, i:i + 1], None, ALU.is_equal))
                then(dve.tensor_tensor(hit[:, 0, :], hit[:, 0, :], hit[:, 1, :], ALU.max))
                then(dve.tensor_tensor(hit[:, 2, :], hit[:, 2, :], hit[:, 3, :], ALU.max))
                then(dve.tensor_scalar(hit[:, 1, :], hit[:, 2, :], -1.0, 1.0, ALU.mult, ALU.add))
                dve.tensor_tensor(ind[0], hit[:, 0, :], hit[:, 1, :], ALU.mult).then_inc(bias_rows, 2)
                dve.tensor_copy(ind[1], hit[:, 2, :]).then_inc(bias_rows, 2)

            def rest_chunk(c, slot, count):
                dve.wait_ge(w_rounded, count)
                raw, ks = raw_chunk(c, slot)
                hi, lo = (wq_hi, wq_lo) if c < HALF else (wo_hi, wo_lo)
                for i, k in enumerate(ks):
                    if c < HALF and has_norm:
                        ins = dve.scalar_tensor_tensor(out=lo[:, k, :], in0=raw[:, i, :], scalar=nw[:, k:k + 1],
                                                       in1=as_f32(hi[:, k, :]), op0=ALU.mult, op1=ALU.subtract)
                    else:
                        ins = dve.tensor_tensor(lo[:, k, :], raw[:, i, :], as_f32(hi[:, k, :]), ALU.subtract)
                ins.then_inc(w_split, 1)

            def mean_square(n):
                dve.wait_ge(ssum_done, n + 1)
                dve.tensor_scalar(ms[:, 0, :], bank(SUMB), 1.0 / C, EPS, ALU.mult, ALU.add).then_inc(ms_step, 1)
                dve.wait_ge(ms_step, 2 * n + 1)
                dve.reciprocal(ms[:, 1, :], ms[:, 0, :]).then_inc(ms_step, 1)

            def take_q(it, t, first=False):
                if has_norm:
                    dve.wait_ge(q_proj, it * T + t + 1)
                    if not first:
                        dve.wait_ge(q_lo, it * T + t)
                    dve.wait_ge(inv_done, it + 1)
                    dve.tensor_tensor(qf[:, :], bank(QB), inv[:, :], ALU.mult).then_inc(q_taken, 1)
                else:
                    dve.wait_ge(q_hi, it * T + t + 1)
                    dve.scalar_tensor_tensor(out=qn_lo[:, :], in0=bank(QB), scalar=scale, in1=as_f32(qn_hi[:, :]),
                                             op0=ALU.mult, op1=ALU.subtract).then_inc(q_lo, 1)

            def reduce_max(it, t, n):
                dve.wait_ge(smax, (it * T + t) * M + n + 1)
                col = n % QT + 32 * (n // QT)
                dve.tensor_reduce(max_cols[:, col:col + 1], bank(MAXB[n % 2]),
                                  AX.X, ALU.max, negate=True).then_inc(reduced, 1)

            if has_norm:
                rest_chunk(0, 0, 1)
                mean_square(0)
            else:
                for c in range(WCH):
                    rest_chunk(c, c % 2, c + 1)
            for t in range(AHEAD):
                take_q(0, t, first=(t == 0))
            for n in range(M):
                reduce_max(0, 0, n)
            with dve.Fori(0, N) as it:
                for t in range(T):
                    for n in range(M):
                        reduce_max(*place(it, t + 1), n)
                        if has_norm and t == SPLIT_AT and n == NS:
                            mean_square(it + 1)
                        if has_norm and t == 0 and n == M // 2:
                            with dve.If(it % B == 0):
                                rest_chunk(1, 0, 2 * (it // B) + 2)
                        if has_norm and t == SPLIT_AT and n == M // 2 + 2:
                            with dve.If(it % B == B - 1):
                                rest_chunk(0, 0, 2 * (it // B) + 3)
                    dve.wait_ge(pv, 1 + (it * T + t + 1) * PV)
                    if t < 2:
                        if not has_norm:
                            dve.wait_ge(stored[t], 1 + it * (2 * DMA))
                    else:
                        dve.wait_ge(o_lo, it * T + t - 1)
                    dve.reciprocal(stage[:, t % 2, :], bank(DENB)).then_inc(recip_done, 1)
                    take_q(*place(it, t + AHEAD))
                    dve.wait_ge(recip_done, it * T + t + 1)
                    dve.tensor_tensor(stage[:, t % 2, :], bank(OUTB), stage[:, t % 2, :], ALU.mult).then_inc(normed, 1)
                for o in range(CK):
                    dve.wait_ge(o_proj, it * CK + o + 1)
                    dve.wait_ge(res_in[o % RS], (it * (CK // RS) + o // RS + 1) * DMA)
                    dve.wait_ge(stored[o % RES], 1 + it * (UR * DMA) + o // RES * DMA)
                    if has_norm:
                        ins = dve.tensor_tensor(results[:, o % RES, :], bank(OB[o]), x_res[:, o % RS, :], ALU.add)
                    else:
                        ins = dve.scalar_tensor_tensor(out=results[:, o % RES, :], in0=bank(OB[o]),
                                                       scalar=bo_cols[:, o:o + 1], in1=x_res[:, o % RS, :],
                                                       op0=ALU.add, op1=ALU.add)
                    ins.then_inc(added, 1)

        @block.tensor
        def _(pe):
            bank_q = q_taken if has_norm else q_lo

            def sum_squares(n):
                pe.wait_ge(sq_step, (n + 1) * SQ)
                pe.matmul(bank(SUMB), ones[:, :], sq[:, 0, :], start=True, stop=True).then_inc(ssum_done, 1)

            def project_q(it, t, first=False):
                if t == 0:
                    pe.wait_ge(x_split, (it + 1) * XC)
                if t == 0 and has_norm:
                    pe.wait_ge(ms_step, 2 * it + 1)
                    if not first:
                        pe.wait_ge(w_split, 2 * (it // B) + 1)
                for k in range(CK):
                    for i, (w, x) in enumerate(((wq_hi, x_hi), (wq_hi, x_lo), (wq_lo, x_hi))):
                        last = pe.matmul(bank(QB), w[:, k, t * P:(t + 1) * P], x[:, k, :],
                                         start=(k == 0 and i == 0), stop=(k == CK - 1 and i == 2))
                last.then_inc(q_proj, 1)

            def maxima(it, t, n):
                s = t % RING
                if n == 0:
                    pe.wait_ge(k_in[s], ring_count(it, t) * (3 * DMA))
                    pe.wait_ge(q_in[s], ring_count(it, t) * (3 * H * DMA))
                elif n >= 2:
                    pe.wait_ge(reduced, (it * T + t) * M + n - 1)
                h, q = n // QT, n % QT
                for p in range(PASS):
                    last = pe.matmul(bank(MAXB[n % 2]), q_ops[0:rows(p), s, h, p, q * P:(q + 1) * P],
                                     k_ops[0:rows(p), s, k_head(h), p, :], start=(p == 0), stop=(p == PASS - 1))
                last.then_inc(smax, 1)

            def turn(it, t):
                pe.wait_ge(reduced, (it * T + t + 1) * M)
                for q in range(QT):
                    last = pe.transpose(ps[:, TURNB, q * P:(q + 1) * P], max_cols[:, q:q + P], ident[:, :])
                last.then_inc(turned, 1)

            def scores(it, t, n):
                s, kt, hp = t % RING, n // (H // 2), n % (H // 2)
                if n == 0:
                    pe.wait_ge(shifted, it * T + t + 1)
                if n >= 2:
                    pe.wait_ge(exped, (it * T + t) * NS + n - 1)
                for j in range(2):
                    h = 2 * hp + j
                    for p in range(PASS):
                        last = pe.matmul(bank(2 * (n % 2) + j), k_ops[:, s, k_head(h), p, kt * P:(kt + 1) * P],
                                         q_ops[:, s, h, p, :], start=(p == 0), stop=(p == PASS - 1))
                last.then_inc(scored, 1)

            def outputs(it, t, kt, part):
                if kt == 0 and part == 0:
                    if kind.shared:
                        if t == 0:
                            pe.wait_ge(v_in, (it + 1) * DMA)
                    else:
                        pe.wait_ge(v_in, (it * T + t + 1) * DMA)
                    pe.wait_ge(normed, 1 + it * T + t)
                pe.wait_ge(exped, (it * T + t) * NS + (kt + 1) * (H // 2))
                for h in range(H):
                    rhs = probs[:, kt * (H // 2) + h // 2, h % 2, :]
                    c0 = (t if kind.shared else h) * d
                    lhs = v[:, kt, c0:c0 + d] if part == 0 else ones[:, 0:d]
                    last = pe.matmul(ps[h * d:(h + 1) * d, OUTB if part == 0 else DENB, :], lhs, rhs,
                                     start=(kt == 0), stop=(kt == KT - 1), skip_group_check=True)
                last.then_inc(pv, 1)

            def project_out(o, tiles):
                for t in tiles:
                    for i, (w, a) in enumerate(((wo_hi, a_hi), (wo_hi, a_lo), (wo_lo, a_hi))):
                        last = pe.matmul(bank(OB[o]), w[:, t, o * P:(o + 1) * P], a[:, t, :],
                                         start=(t == 0 and i == 0), stop=(t == T - 1 and i == 2))
                if T - 1 in tiles:
                    last.then_inc(o_proj, 1)

            pe.wait_ge(consts, 2)
            pe.wait_ge(consts_v, 5)
            if has_norm:
                sum_squares(0)
                pe.wait_ge(w_split, 1)
            else:
                pe.wait_ge(w_split, WCH)
                pe.wait_ge(rows_set, 6 * H * RING * DMA)
            for t in range(AHEAD):
                if t > 0:
                    pe.wait_ge(bank_q, t)
                project_q(0, t, first=(t == 0))
            for n in range(M):
                if n == 1:
                    pe.wait_ge(bank_q, AHEAD)
                maxima(0, 0, n)
            turn(0, 0)
            with pe.Fori(0, N) as it:
                for t in range(T):
                    pieces = [(kt, part) for kt in range(KT) for part in range(2)]
                    for n in range(H // 2):
                        if t == 0 and n == 1:
                            pe.wait_ge(added, 1 + it * CK)
                        scores(it, t, n)
                    if t == 0 and H == 2:
                        pe.wait_ge(added, 1 + it * CK)
                    for r in range(NS):
                        maxima(*place(it, t + 1), 2 * r)
                        if r == 0:
                            pe.wait_ge(bank_q, it * T + t + AHEAD)
                        summing = has_norm and t == SPLIT_AT and r == NS // 2
                        if summing:
                            pe.wait_ge(reduced, (it * T + t + 1) * M + 2 * r)
                            sum_squares(it + 1)
                        else:
                            maxima(*place(it, t + 1), 2 * r + 1)
                        if H // 2 + r < NS:
                            scores(it, t, H // 2 + r)
                        upto = min((r + 1) * (PV // NS) if H == 2 else r, PV - 1)
                        while PV - len(pieces) < upto:
                            outputs(it, t, *pieces.pop(0))
                        if summing:
                            pe.wait_ge(ms_step, 2 * it + 3)
                            maxima(*place(it, t + 1), 2 * r + 1)
                    turn(*place(it, t + 1))
                    for piece in pieces:
                        outputs(it, t, *piece)
                    project_q(*place(it, t + AHEAD))
                if has_norm:
                    pe.wait_ge(w_split, 2 * (it // B) + 2)
                pe.wait_ge(o_lo, (it + 1) * T - 1)
                pe.wait_ge(shifted, (it + 1) * T + 1)
                project_out(0, range(T - 1))
                pe.wait_ge(bank_q, (it + 1) * T + AHEAD)
                project_out(1, range(T - 1))
                pe.wait_ge(o_lo, (it + 1) * T)
                project_out(0, [T - 1])
                project_out(1, [T - 1])
                pe.wait_ge(exped, (it + 1) * (T * NS))
                for o in range(2, CK):
                    project_out(o, range(T))


def build(nc, a, out):
    k_scratch = nc.dram_tensor("k_scratch", (B, PROJ // P, 2, P, S), F32, kind="Internal").ap()
    v_scratch = nc.dram_tensor("v_scratch", (B, KT, P, PROJ), F32, kind="Internal").ap()
    project_context(nc, "kp", a["ctx_t"], a["wk"], k_scratch, True)
    project_context(nc, "vp", a["ctx_t"], a["wv"], v_scratch, False)
    bias = dict(bo=a["bo"], mask_a=a["mask_a"], mask_b=a["mask_b"], tok_a=a["tok_a"], tok_b=a["tok_b"])
    attention_layers(nc, "a0", Kind(1, INNER0, 64, False), a["x_t"], out, k_scratch, v_scratch,
                     a["wq0"], a["wo0"], bias=bias)
    attention_layers(nc, "a1", Kind(LAYERS, INNER, 32, True), out, out, k_scratch, v_scratch,
                     a["wq"], a["wo"], norm_w=a["norm_w"])


def kernel(**inputs):
    import numpy as np
    import concourse.bacc as bacc
    from concourse.bass_utils import run_bass_kernel_spmd

    own = range(1, LAYERS + 1)
    arrays = {
        "x_t": inputs["x"].transpose(0, 2, 1),
        "ctx_t": inputs["ctx_2048"].transpose(0, 2, 1),
        "wk": np.concatenate([inputs["L0_xattn_Wk"]] + [inputs[f"L{i}_xattn_wk"] for i in own], axis=1),
        "wv": np.concatenate([inputs["L0_xattn_Wv"]] + [inputs[f"L{i}_xattn_wv"] for i in own], axis=1),
        "wq0": inputs["L0_xattn_Wq"][None],
        "wo0": inputs["L0_xattn_Wo"][None],
        "wq": np.stack([inputs[f"L{i}_xattn_wq"] for i in own]),
        "wo": np.stack([inputs[f"L{i}_xattn_wo"] for i in own]),
        "norm_w": np.stack([inputs[f"L{i}_xattn_norm_w"].reshape(CK, P).T for i in own]),
        "bo": inputs["L0_xattn_bo"].reshape(CK, P).T,
        "mask_a": inputs["mask_S_fk1"],
        "mask_b": inputs["mask_S_fk0"],
        "tok_a": inputs["L0_xattn_token_indices_A"],
        "tok_b": inputs["L0_xattn_token_indices_B"],
    }
    arrays = {n: np.ascontiguousarray(x) for n, x in arrays.items()}
    nc = bacc.Bacc("TRN2", target_bir_lowering=False, num_devices=1)
    aps = {n: nc.dram_tensor(f"in_{n}", x.shape, mybir.dt.from_np(x.dtype), kind="ExternalInput").ap()
           for n, x in arrays.items()}
    out = nc.dram_tensor("out_t", (B, C, S), F32, kind="ExternalOutput").ap()
    build(nc, aps, out)
    r = run_bass_kernel_spmd(nc, [{f"in_{n}": x for n, x in arrays.items()}], core_ids=[0])
    return np.ascontiguousarray(r.results[0]["out_t"].transpose(0, 2, 1))
```

```python
from contextlib import ExitStack, contextmanager

import concourse.bass as bass
from concourse import mybir

P = 128
W = 512
F32 = mybir.dt.float32
F32R = mybir.dt.float32r
I32 = mybir.dt.int32
ALU = mybir.AluOpType
ACT = mybir.ActivationFunctionType
AX = mybir.AxisListType

B = 8
C = 512
CT = 1024
S = 512
INNER0 = 1024
INNER = 512
KV = 128
LAYERS = 3
PROJ = INNER0 + LAYERS * KV
KT = S // P
QT = S // P
CK = C // P
EPS = 1e-5
SUPPRESS = 20.0
DMA = 16
SHIFT = 96
BIAS = 64



def as_f32(ap):
    return ap.bitcast(F32)


def project_context(nc, name, ctx_t, weights, scratch, is_k):
    KC = CT // P
    VP = 3
    WB = PROJ // P if is_k else KT * VP
    NCH = KC // 2
    RAW = 4
    CHUNK_AT = {2 * j + 1: j for j in range(NCH)}
    with ExitStack() as mem:
        def sb(n, shape, dt):
            return mem.enter_context(nc.sbuf_tensor(f"{name}_{n}", shape, dt))

        def sem(n):
            return mem.enter_context(nc.semaphore(f"{name}_{n}"))

        w_hi = sb("w_hi", [P, KC, PROJ], F32R)
        w_lo = sb("w_lo", [P, KC, PROJ], F32R)
        c_hi = [sb(f"c_hi{i}", [P, KC, S], F32R) for i in range(2)]
        c_lo = [sb(f"c_lo{i}", [P, KC, S], F32R) for i in range(2)]
        raw = sb("raw", [P, RAW, PROJ], F32)
        out = [sb(f"out{i}", [P, 2, W], F32R) if is_k else sb(f"out{i}", [P, 1, W], F32) for i in range(2)]
        ps = mem.enter_context(nc.psum_tensor(f"{name}_ps", [P, 2, W], F32))

        raw_in = [sem(f"raw_in{i}") for i in range(RAW)]
        hi_done = sem("hi_done")
        lo_done = sem("lo_done")
        block_done = sem("block_done")
        out_hi = sem("out_hi")
        out_lo = sem("out_lo")
        stored = [sem(f"stored{i}") for i in range(2)]

        w_rows = weights.rearrange("(k p) n -> p k n", p=P)
        taken = out_lo if is_k else out_hi

        def chunk_view(j):
            return raw[:, j % RAW, 0:2 * S].rearrange("p (k s) -> p k s", k=2)

        def width(n):
            return W if is_k or n % VP < 2 else LAYERS * KV

        def raw_count(b, j):
            return b * (DMA * NCH // RAW) + DMA * (KC // RAW + j // RAW + 1)

        block = mem.enter_context(nc.Block())

        @block.gpsimd
        def _(pool):
            for credit in (taken, *stored):
                pool.sem_inc(credit, 1)

        @block.sync
        def _(sp):
            def load(b, place, j):
                sp.wait_ge(lo_done, place * NCH + KC + j + 1 - RAW)
                src = ctx_t[b].rearrange("(k p) s -> p k s", p=P)
                sp.dma_start(chunk_view(j), src[:, 2 * j:2 * j + 2, :]).then_inc(raw_in[j % RAW], DMA)

            for k in range(KC):
                if k >= RAW:
                    sp.wait_ge(lo_done, k + 1 - RAW)
                sp.dma_start(raw[:, k % RAW, :], w_rows[:, k, :]).then_inc(raw_in[k % RAW], DMA)
            for j in range(NCH):
                load(0, 0, j)
            with sp.Fori(0, B // 2) as bb:
                for par in range(2):
                    b = bb * 2 + par
                    for n in range(WB):
                        m = par * WB + n
                        sp.wait_ge(taken, 1 + b * WB + n + 1)
                        if is_k:
                            dst = scratch[b, n].rearrange("c p s -> p c s")
                        else:
                            dst = scratch[b, n // VP][:, (n % VP) * W:(n % VP) * W + width(n)]\
                                .rearrange("p (c s) -> p c s", c=1)
                        src = out[m % 2][:, :, 0:width(n)]
                        sp.dma_start(dst, as_f32(src) if is_k else src).then_inc(stored[m % 2], DMA)
                        if n in CHUNK_AT:
                            load((b + 1) % B, b + 1, CHUNK_AT[n])
            for i in range(2):
                sp.wait_ge(stored[i], 1 + DMA * WB * B // 2)

        @block.scalar
        def _(act):
            def round_chunk(place, par, j):
                act.wait_ge(raw_in[j % RAW], raw_count(place, j))
                act.activation(c_hi[par][:, 2 * j:2 * j + 2, :], chunk_view(j), ACT.Copy).then_inc(hi_done, 1)

            for k in range(KC):
                act.wait_ge(raw_in[k % RAW], DMA * (k // RAW + 1))
                act.activation(w_hi[:, k, :], raw[:, k % RAW, :], ACT.Copy).then_inc(hi_done, 1)
            for j in range(NCH):
                round_chunk(0, 0, j)
            with act.Fori(0, B // 2) as bb:
                for par in range(2):
                    b = bb * 2 + par
                    for n in range(WB):
                        m = par * WB + n
                        w = width(n)
                        act.wait_ge(block_done, b * WB + n + 1)
                        act.wait_ge(stored[m % 2], 1 + bb * (DMA * WB) + DMA * (m // 2))
                        act.activation(out[m % 2][:, 0, 0:w], ps[:, m % 2, 0:w], ACT.Copy).then_inc(out_hi, 1)
                        if n in CHUNK_AT:
                            round_chunk(b + 1, 1 - par, CHUNK_AT[n])

        @block.vector
        def _(dve):
            def rest_chunk(place, par, j):
                dve.wait_ge(hi_done, place * NCH + KC + j + 1)
                dve.tensor_tensor(c_lo[par][:, 2 * j:2 * j + 2, :], chunk_view(j),
                                  as_f32(c_hi[par][:, 2 * j:2 * j + 2, :]), ALU.subtract).then_inc(lo_done, 1)

            for k in range(KC):
                dve.wait_ge(hi_done, k + 1)
                dve.tensor_tensor(w_lo[:, k, :], raw[:, k % RAW, :], as_f32(w_hi[:, k, :]), ALU.subtract)\
                    .then_inc(lo_done, 1)
            for j in range(NCH):
                rest_chunk(0, 0, j)
            with dve.Fori(0, B // 2) as bb:
                for par in range(2):
                    b = bb * 2 + par
                    for n in range(WB):
                        m = par * WB + n
                        if is_k:
                            dve.wait_ge(out_hi, b * WB + n + 1)
                            dve.tensor_tensor(out[m % 2][:, 1, :], ps[:, m % 2, :], as_f32(out[m % 2][:, 0, :]),
                                              ALU.subtract).then_inc(out_lo, 1)
                        if n in CHUNK_AT:
                            rest_chunk(b + 1, 1 - par, CHUNK_AT[n])

        @block.tensor
        def _(pe):
            with pe.Fori(0, B // 2) as bb:
                for par in range(2):
                    b = bb * 2 + par
                    pe.wait_ge(lo_done, (b + 1) * NCH + KC)
                    for n in range(WB):
                        m = par * WB + n
                        if par == 0 and n < 2:
                            pe.wait_ge(taken, 1 + b * WB)
                        else:
                            pe.wait_ge(taken, 1 + b * WB + n - 1)
                        for k in range(KC):
                            if is_k:
                                pairs = [(w, c[par][:, k, :]) for w, c in ((w_hi, c_hi), (w_hi, c_lo), (w_lo, c_hi))]
                                pairs = [(w[:, k, n * P:(n + 1) * P], c) for w, c in pairs]
                            else:
                                t, c0 = n // VP, (n % VP) * W
                                pairs = [(c[par][:, k, t * P:(t + 1) * P], w[:, k, c0:c0 + width(n)])
                                         for c, w in ((c_hi, w_hi), (c_hi, w_lo), (c_lo, w_hi))]
                            for i, (stationary, moving) in enumerate(pairs):
                                last = pe.matmul(ps[:, m % 2, 0:width(n)], stationary, moving,
                                                 start=(k == 0 and i == 0), stop=(k == KC - 1 and i == 2))
                        last.then_inc(block_done, 1)


class Kind:

    def __init__(self, layers, inner, head, shared_kv):
        self.layers = layers
        self.d = head
        self.T = inner // P
        self.H = P // head
        self.shared = shared_kv
        self.PASS = 4 * head // P
        self.NS = self.H // 2 * KT
        self.M = self.H * QT
        self.KHEADS = 1 if shared_kv else self.H
        assert self.M == 2 * self.NS and self.T % RING == 0


RING = 4
AHEAD = 3


def attention_layers(nc, name, kind, x_in, x_out, k_scratch, v_scratch, wq, wo, norm_w=None, bias=None):
    L, d, T, H, NS, M, PASS = kind.layers, kind.d, kind.T, kind.H, kind.NS, kind.M, kind.PASS
    N = L * B
    has_norm = norm_w is not None
    scale = d ** -0.5
    UT = T // RING
    PRE = (KT - 1, KT - 2) if has_norm else (KT,)
    SUMS = sum(PRE) - len(PRE)
    LATE = 1 if has_norm else 0
    XAT = (M - 1,) if has_norm else (3, M - 1)
    OUT_AT = (2, 3, 5, NS - 1) if has_norm else (1, 2, 3)
    PARTS, EARLY = 4, (3 if has_norm else 2)
    SPLIT_AT = T - AHEAD
    XT = CK if has_norm else CK // 2
    XC = CK // XT
    SQ = CK
    MS = 1 + PARTS
    EARLIER = 1 if has_norm else 0
    LOAD_AT = 2 if has_norm else 0
    RS = 4 if kind.shared else 1
    RES = 4 if kind.shared else 2
    UR = CK // RES
    with ExitStack() as mem:
        def sb(n, shape, dt):
            return mem.enter_context(nc.sbuf_tensor(f"{name}_{n}", shape, dt))

        def sem(n):
            return mem.enter_context(nc.semaphore(f"{name}_{n}"))

        wq_hi = sb("wq_hi", [P, CK, T * P], F32R)
        wq_lo = sb("wq_lo", [P, CK, T * P], F32R)
        wo_hi = sb("wo_hi", [P, T, C], F32R)
        wo_lo = sb("wo_lo", [P, T, C], F32R)
        x_hi = sb("x_hi", [P, CK, S], F32R)
        x_lo = sb("x_lo", [P, CK, S], F32R)
        x_raw = sb("x_raw", [P, XT, S], F32)
        x_res = sb("x_res", [P, RS, S], F32) if has_norm else x_raw[:, 1:2, :]
        qn_hi = sb("qn_hi", [P, S], F32R)
        qn_lo = sb("qn_lo", [P, S], F32R)
        a_hi = sb("a_hi", [P, T, S], F32R)
        a_lo = sb("a_lo", [P, T, S], F32R)
        q_ops = sb("q_ops", [P, RING, H, PASS, S], F32R)
        k_ops = sb("k_ops", [P, RING, kind.KHEADS, PASS, S], F32R)
        v = sb("v", [P, KT, P], F32)
        probs = sb("probs", [P, NS, 2, S], F32)
        sums = sb("sums", [P, H // 2, 2, S], F32) if has_norm else probs[:, 0:H // 2]
        stage = sb("stage", [P, 2, S], F32)
        results = sb("results", [P, RES, S], F32) if has_norm else stage
        max_cols = sb("max_cols", [P, P + QT], F32)
        ident = sb("ident", [P, P], F32)
        ones = sb("ones", [P, P if has_norm else d], F32)
        if has_norm:
            w_raw = sb("w_raw", [P, 1, 4 * W], F32)
            qf = sb("qf", [P, S], F32)
            inv = sb("inv", [P, S], F32)
            sq = sb("sq", [P, CK, S], F32)
            ms = sb("ms", [P, 2, S], F32)
            nw = sb("nw", [P, CK], F32)
        else:
            w_raw = probs[:, 0:4].rearrange("p (a b) c s -> p a (b c s)", a=2)
            bo_cols = sb("bo_cols", [P, C // P], F32)
            spare = probs[:, 0:4].rearrange("p a c s -> p (a c) s")
            hit = spare[0:1, 0:4, :]
            mrow, brow = spare[0:2, 4, :], spare[0:2, 5, :]
            key_no, key_no_i = spare[0:1, 6, :], spare[0:1, 7, :].bitcast(I32)
            b_hi, b_lo = brow.bitcast(F32R), stage[0:2, 0, :].bitcast(F32R)
            ind = [stage[0:1, 1, :].bitcast(F32R), key_no.bitcast(F32R)]
            tok_i = v[0:1, 0, 0:4].bitcast(I32)
            tok, tok_w = v[0:1, 0, 4:8], v[0:1, 0, 8:12]
        ps = mem.enter_context(nc.psum_tensor(f"{name}_ps", [P, 8, W], F32))
        OUTB, DENB = 6, 7
        TURNB, QB = 4, 5
        MAXB = (4, 5, 4, 5, 7, 4, 5, 7, 4, 5, 7, 4, 5, 4, 5, 4) if has_norm else (4, 5, 4, 5, 7, 4, 5, 4)
        SUMB = MAXB[(NS + 1) % M]
        OB = (4, 5, 2, 3)

        consts = sem("consts")
        consts_v = sem("consts_v")
        rows_in = sem("rows_in")
        brow_step = sem("brow_step")
        bias_rows = sem("bias_rows")
        rows_set = sem("rows_set")
        w_in = [sem(f"w_in{i}") for i in range(2)]
        nw_in = sem("nw_in")
        w_rounded = sem("w_rounded")
        w_split = sem("w_split")
        x_in_s = sem("x_in")
        x_hi_done = sem("x_hi_done")
        x_split = sem("x_split")
        sq_step = sem("sq_step")
        ssum_done = sem("ssum_done")
        ms_step = sem("ms_step")
        inv_done = sem("inv_done")
        q_proj = sem("q_proj")
        q_taken = sem("q_taken")
        q_hi = sem("q_hi")
        q_lo = sem("q_lo")
        q_in = [sem(f"q_in{i}") for i in range(RING)]
        k_in = [sem(f"k_in{i}") for i in range(RING)]
        v_in = sem("v_in")
        smax = sem("smax")
        reduced = sem("reduced")
        turned = sem("turned")
        shifted = sem("shifted")
        scored = sem("scored")
        exped = sem("exped")
        pv = sem("pv")
        summed = sem("summed")
        den_done = sem("den_done")
        recip_done = sem("recip_done")
        normed = sem("normed")
        o_hi = sem("o_hi")
        o_lo = sem("o_lo")
        o_proj = sem("o_proj")
        res_in = [sem(f"res_in{i}") for i in range(RS)]
        added = sem("added")
        stored = [sem(f"stored{i}") for i in range(RES)]

        def bank(i):
            return ps[:, i, :]

        def last_use(n):
            return max(m for m in range(n) if MAXB[m] == MAXB[n])

        def k_head(h):
            return 0 if kind.shared else h

        def rows(p):
            return SHIFT if p == PASS - 1 else P

        def place(it, t):
            return (it + 1, t - T) if t >= T else (it, t)

        def ring_count(it, t):
            return it * UT + t // RING + 1

        WCH = 2 * T * P * CK // (4 * W)
        HALF = WCH // 2

        def chunk(w, c):
            src = w.rearrange("(k p) n -> p k n", p=P)
            n = src.shape[1] // HALF
            return src[:, (c % HALF) * n:(c % HALF + 1) * n, :]

        def raw_chunk(c, slot):
            n = (CK if c < HALF else T) // HALF
            return w_raw[:, slot, :].rearrange("p (k n) -> p k n", k=n), range((c % HALF) * n, (c % HALF + 1) * n)

        block = mem.enter_context(nc.Block())
        X0 = P - d

        @block.sync
        def _(sp):
            def load_k(it, t, n=None):
                s = t % RING
                b, l = (0, 0) if n is None else (n % B, n // B)
                for i, part in enumerate((0, 1, 0)):
                    at = (i * d) % P
                    dst = as_f32(k_ops[at:at + d, s, :, (i * d) // P, :])
                    if kind.shared:
                        src = k_scratch[b, INNER0 // P + l, part][t * d:(t + 1) * d, :]
                        src = src.rearrange("(h p) s -> p h s", h=1)
                    else:
                        src = k_scratch[b, t, part].rearrange("(h p) s -> p h s", h=H)
                    sp.dma_start(dst, src).then_inc(k_in[s], DMA)

            def load_q(it, t):
                s = t % RING
                sp.wait_ge(q_lo, it * T + t + 1)
                for h in range(H):
                    for i, part in enumerate((qn_hi, qn_hi, qn_lo)):
                        at = (i * d) % P
                        sp.dma_start(as_f32(q_ops[at:at + d, s, h, (i * d) // P, :]),
                                     as_f32(part[h * d:(h + 1) * d, :])).then_inc(q_in[s], DMA)

            def load_v(t, n=None):
                b, l = (0, 0) if n is None else (n % B, n // B)
                src = v_scratch[b].rearrange("k p n -> p k n")
                if kind.shared:
                    sp.dma_start(v[:, :, :], src[:, :, bass.ds(INNER0 + l * KV, KV)]).then_inc(v_in, DMA)
                else:
                    sp.dma_start(v[:, :, :], src[:, :, t * P:(t + 1) * P]).then_inc(v_in, DMA)

            def load_x(b, c):
                src = x_in[b].rearrange("(k p) s -> p k s", p=P)[:, c * XT:(c + 1) * XT, :]
                sp.dma_start(x_raw[:, :, :], src).then_inc(x_in_s, DMA)

            load_x(0, 0)
            if has_norm:
                sp.dma_start(nw[:, :], norm_w[0]).then_inc(nw_in, DMA)
                sp.dma_start(w_raw[:, 0, :].rearrange("p (k n) -> p k n", k=CK), chunk(wq[0], 0)).then_inc(w_in[0], DMA)
            else:
                sp.dma_start(bo_cols[:, :], bias["bo"]).then_inc(rows_in, DMA)
                for i, m in enumerate(("mask_a", "mask_b")):
                    sp.dma_start(spare[i:i + 1, 4, :], bias[m].rearrange("(a s) -> a s", a=1)).then_inc(rows_in, DMA)
                for i, m in enumerate(("tok_a", "tok_b")):
                    sp.dma_start(tok_i[:, 2 * i:2 * i + 2], bias[m].rearrange("(a s) -> a s", a=1))\
                        .then_inc(rows_in, DMA)
                for t in range(AHEAD):
                    load_k(0, t)
                sp.wait_ge(bias_rows, 6)
                sp.wait_ge(consts_v, 4)
                sp.wait_ge(consts, 4)
                sp.dma_start(raw_chunk(0, 0)[0], chunk(wq[0], 0)).then_inc(w_in[0], DMA)
                def spread(row):
                    n = row.shape[0]
                    return as_f32(row).rearrange("r (a s) -> r a s", a=1).broadcast_to((n, RING * H, S))

                q_rows = as_f32(q_ops[:, :, :, PASS - 1, :]).rearrange("p s h n -> p (s h) n")
                k_rows = as_f32(k_ops[:, :, :, PASS - 1, :]).rearrange("p s h n -> p (s h) n")
                sp.dma_start(q_rows[BIAS:BIAS + 2], spread(b_hi)).then_inc(rows_set, DMA)
                sp.dma_start(q_rows[BIAS + 2:BIAS + 4], spread(b_lo)).then_inc(rows_set, DMA)
                for i in range(4):
                    sp.dma_start(k_rows[BIAS + i:BIAS + i + 1], spread(ind[i % 2])).then_inc(rows_set, DMA)
                sp.wait_ge(rows_set, 6 * DMA)
                for c in range(1, WCH):
                    if c >= 2:
                        sp.wait_ge(w_split, c - 1)
                    if 2 <= c <= XC:
                        sp.wait_ge(x_split, c - 1)
                        load_x(0, c - 1)
                    dst, ks = raw_chunk(c, c % 2)
                    sp.dma_start(dst, chunk((wq if c < HALF else wo)[0], c)).then_inc(w_in[c % 2], DMA)
            if has_norm:
                for t in range(AHEAD):
                    load_k(0, t)
            load_v(0)
            if has_norm:
                sp.wait_ge(x_split, 1)
                sp.wait_ge(sq_step, 1)
                load_x(1, 0)
                sp.wait_ge(w_split, 1)
                sp.dma_start(w_raw[:, 0, :].rearrange("p (k n) -> p k n", k=T), chunk(wo[0], 1))\
                    .then_inc(w_in[0], DMA)
            for t in range(AHEAD):
                load_q(0, t)
            with sp.Fori(0, N) as it:
                nxt = (it + 1) % N
                for t in range(T):
                    sp.wait_ge(scored, 1 + (it * T + t) * NS)
                    it_q, t_q = place(it, t + AHEAD)
                    load_k(it_q, t_q, it if t + AHEAD < T else nxt)
                    if t == LOAD_AT:
                        sp.wait_ge(x_split, (it + 1 + EARLIER) * XC)
                        for i in range(RES):
                            sp.wait_ge(stored[i], 1 + it * (UR * DMA))
                        load_x((it + 1 + EARLIER) % B, 0)
                    if t == 0 and has_norm:
                        with sp.If(it % B == B - 1):
                            sp.wait_ge(w_split, 2 * (it // B) + 2)
                            sp.dma_start(w_raw[:, 0, :].rearrange("p (k n) -> p k n", k=CK),
                                         chunk(wq[nxt // B], 0)).then_inc(w_in[0], DMA)
                            sp.dma_start(nw[:, :], norm_w[nxt // B]).then_inc(nw_in, DMA)
                    if t == LOAD_AT and has_norm:
                        with sp.If(it % B == B - 1):
                            sp.wait_ge(w_split, 2 * (it // B) + 3)
                            sp.dma_start(w_raw[:, 0, :].rearrange("p (k n) -> p k n", k=T),
                                         chunk(wo[nxt // B], 1)).then_inc(w_in[0], DMA)
                    if t == SPLIT_AT:
                        for c in range(1, XC):
                            sp.wait_ge(x_split, (it + 1) * XC + c)
                            load_x(nxt % B, c)
                    if t == T - 1:
                        src = x_in[it % B]
                        sp.wait_ge(added, CK + it * CK)
                        if not has_norm:
                            sp.wait_ge(x_split, (it + 2) * XC)
                        for o in range(RS):
                            sp.dma_start(x_res[:, o, :], src[o * P:(o + 1) * P, :]).then_inc(res_in[o], DMA)
                    if not kind.shared:
                        sp.wait_ge(pv, 1 + (it * T + t + 1) * KT)
                        load_v((t + 1) % T, it if t + 1 < T else nxt)
                    if t < T - 1:
                        load_q(it_q, t_q)
                if kind.shared:
                    sp.wait_ge(pv, 1 + (it + 1) * (T * KT))
                    load_v(0, nxt)
                for o in range(CK):
                    sp.wait_ge(added, CK + it * CK + o + 1)
                    sp.dma_start(x_out[it % B][o * P:(o + 1) * P, :], results[:, o % RES, :])\
                        .then_inc(stored[o % RES], DMA)
                    if o + RS < CK:
                        sp.dma_start(x_res[:, (o + RS) % RS, :],
                                     x_in[it % B][(o + RS) * P:(o + RS + 1) * P, :])\
                            .then_inc(res_in[(o + RS) % RS], DMA)
                load_q(it + 1, AHEAD - 1)
            for i in range(RES):
                sp.wait_ge(stored[i], 1 + N * UR * DMA)
            sp.wait_ge(x_in_s, (N + 1 + EARLIER) * XC * DMA)
            if has_norm:
                sp.wait_ge(w_in[0], (2 * L + 2) * DMA)
                sp.wait_ge(nw_in, (L + 1) * DMA)
            for t in range(AHEAD):
                sp.wait_ge(k_in[t], ring_count(N, t) * (3 * DMA))
                sp.wait_ge(q_in[t], ring_count(N, t) * (3 * H * DMA))
            sp.wait_ge(v_in, (N + 1 if kind.shared else N * T + 1) * DMA)

        @block.gpsimd
        def _(pool):
            for credit in (scored, pv, normed, *stored):
                pool.sem_inc(credit, 1)
            pool.sem_inc(added, CK)
            pool.memset(ident[:, :], 0.0).then_inc(consts, 1)
            pool.wait_ge(consts, 1)
            pool.affine_select(out=ident[:, :], in_=ident[:, :], compare_op=ALU.not_equal, fill=1.0, base=0,
                               pattern=[[-1, P]], channel_multiplier=1).then_inc(consts, 1)
            if not has_norm:
                pool.iota(key_no_i, pattern=[[1, S]], base=0, channel_multiplier=0).then_inc(consts, 1)
                pool.wait_ge(consts, 3)
                pool.memset(as_f32(k_ops[X0:SHIFT, :, :, PASS - 1, :]), 0.0).then_inc(consts, 1)
            def sum_squares(n):
                for k in range(1, CK):
                    pool.wait_ge(sq_step, n * SQ + k)
                    pool.tensor_tensor(sq[:, 0, :], sq[:, 0, :], sq[:, k, :], ALU.add).then_inc(sq_step, 1)

            def sum_probs(it, t):
                for i in range(1, max(PRE)):
                    for hp in (hp for hp in range(H // 2) if i < PRE[hp]):
                        n = i * (H // 2) + hp
                        if n == H // 2 and not has_norm:
                            pool.wait_ge(pv, 1 + (it * T + t) * KT + 1)
                        if i > 1:
                            pool.wait_ge(summed, (it * T + t) * SUMS + n - H + 1)
                        pool.wait_ge(exped, (it * T + t) * NS + n + 1)
                        pool.tensor_tensor(sums[:, hp], (probs if i == 1 else sums)[:, hp], probs[:, n], ALU.add)\
                            .then_inc(summed, 1)

            def rest_q(it, t):
                if has_norm:
                    pool.wait_ge(q_hi, it * T + t + 1)
                    pool.tensor_tensor(qn_lo[:, :], qf[:, :], as_f32(qn_hi[:, :]), ALU.subtract).then_inc(q_lo, 1)

            def rest_output(it, t):
                pool.wait_ge(o_hi, it * T + t + 1)
                pool.tensor_tensor(a_lo[:, t, :], stage[:, t % 2, :], as_f32(a_hi[:, t, :]), ALU.subtract)\
                    .then_inc(o_lo, 1)

            if has_norm:
                sum_squares(0)
            for t in range(AHEAD):
                rest_q(0, t)
            if has_norm:
                sum_squares(1)
            with pool.Fori(0, N) as it:
                for t in range(T):
                    sum_probs(it, t)
                    if t > 0:
                        rest_output(it, t - 1)
                    if t == T - 1:
                        rest_output(it, t)
                    if has_norm and t == T - 1:
                        sum_squares(it + 2)
                    rest_q(*place(it, t + AHEAD))

        @block.scalar
        def _(act):
            def round_chunk(c, slot, count, l=0):
                act.wait_ge(w_in[slot], count * DMA)
                raw, ks = raw_chunk(c, slot)
                if c < HALF and has_norm:
                    act.wait_ge(nw_in, (l + 1) * DMA)
                for i, k in enumerate(ks):
                    if c < HALF and has_norm:
                        ins = act.activation(wq_hi[:, k, :], raw[:, i, :], ACT.Copy, scale=nw[:, k:k + 1])
                    else:
                        ins = act.activation((wq_hi if c < HALF else wo_hi)[:, k, :], raw[:, i, :], ACT.Copy)
                ins.then_inc(w_rounded, 1)

            def round_x(n, c):
                act.wait_ge(x_in_s, (n * XC + c + 1) * DMA)
                act.activation(x_hi[:, c * XT:(c + 1) * XT, :], x_raw[:, :, :], ACT.Copy).then_inc(x_hi_done, 1)

            def squares(n):
                act.wait_ge(x_in_s, (n + 1) * DMA)
                act.activation(sq[:, :, :], x_raw[:, :, :], ACT.Square).then_inc(sq_step, 1)

            def inv_rms(n):
                act.wait_ge(ms_step, MS * (n + 1))
                act.activation(inv[:, :], ms[:, 1, :], ACT.Sqrt, scale=scale * scale).then_inc(inv_done, 1)

            def round_q(it, t, first=False):
                if has_norm:
                    act.wait_ge(q_taken, it * T + t + 1)
                else:
                    act.wait_ge(q_proj, it * T + t + 1)
                if not first:
                    it_p, t_p = (it, t - 1) if t > 0 else (it - 1, T - 1)
                    act.wait_ge(q_in[t_p % RING], ring_count(it_p, t_p) * (3 * H * DMA))
                if has_norm:
                    act.activation(qn_hi[:, :], qf[:, :], ACT.Copy).then_inc(q_hi, 1)
                else:
                    act.activation(qn_hi[:, :], bank(QB), ACT.Copy, scale=scale).then_inc(q_hi, 1)

            def shift(it, t):
                act.wait_ge(turned, it * T + t + 1)
                for h in range(H):
                    ins = act.activation(q_ops[SHIFT:SHIFT + 1, t % RING, h, PASS - 1, :],
                                         ps[32 * h:32 * h + 1, TURNB, :], ACT.Copy)
                ins.then_inc(shifted, 1)

            def round_output(it, t):
                act.wait_ge(normed, 1 + it * T + t + 1)
                act.activation(a_hi[:, t, :], stage[:, t % 2, :], ACT.Copy).then_inc(o_hi, 1)

            if has_norm:
                round_x(0, 0)
                squares(0)
                round_chunk(0, 0, 1)
                inv_rms(0)
            else:
                for c in range(HALF):
                    round_chunk(c, c % 2, c // 2 + 1)
                    if c < XC:
                        round_x(0, c)
            for t in range(AHEAD - LATE):
                round_q(0, t, first=(t == 0))
                if not has_norm and HALF + t < WCH:
                    round_chunk(HALF + t, (HALF + t) % 2, (HALF + t) // 2 + 1)
            if not has_norm:
                act.wait_ge(w_split, WCH)
            shift(0, 0)
            if has_norm:
                squares(1)
            with act.Fori(0, N) as it:
                for t in range(T):
                    for s in range(NS):
                        act.wait_ge(scored, 1 + (it * T + t) * NS + s + 1)
                        act.activation(probs[:, s], ps[:, 2 * (s % 2):2 * (s % 2) + 2, :], ACT.Exp)\
                            .then_inc(exped, 1)
                        if t == SPLIT_AT and s in ((3,) if has_norm else (1, 3)):
                            round_x(it + 1, 0 if has_norm else s // 2)
                        if has_norm and t == T - 1 and s == NS - 1:
                            squares(it + 2)
                        if has_norm and t == 1 and s == NS - 1:
                            act.wait_ge(q_taken, (it + 1) * T)
                            inv_rms(it + 1)
                        if has_norm and s == 1:
                            round_q(*place(it, t - 1 + AHEAD))
                        if t > 0 and s == NS // 2:
                            round_output(it, t - 1)
                        if has_norm and t == 0 and s == NS // 2:
                            with act.If(it % B == 0):
                                round_chunk(1, 0, 2 * (it // B) + 2)
                        if has_norm and t == SPLIT_AT and s == NS // 2:
                            with act.If(it % B == B - 1):
                                round_chunk(0, 0, 2 * (it // B) + 3, it // B + 1)
                    shift(*place(it, t + 1))
                    if not has_norm:
                        round_q(*place(it, t + AHEAD))
                    if t == T - 1:
                        round_output(it, t)
            if has_norm:
                round_q(N, AHEAD - 1)

        @block.vector
        def _(dve):
            dve.memset(max_cols[:, :], 0.0).then_inc(consts_v, 1)
            dve.memset(ones[:, :], 1.0).then_inc(consts_v, 1)
            dve.memset(as_f32(q_ops[X0:P, :, :, PASS - 1, :]), 0.0).then_inc(consts_v, 1)
            dve.memset(as_f32(k_ops[SHIFT:P, :, :, PASS - 1, :]), 1.0).then_inc(consts_v, 1)
            if not has_norm:
                dve.wait_ge(rows_in, 5 * DMA)
                dve.wait_ge(consts, 4)
                step = [0]

                def then(ins):
                    step[0] += 1
                    ins.then_inc(brow_step, 1)
                    dve.wait_ge(brow_step, step[0])

                then(dve.tensor_scalar(brow, mrow, -1.0, 1.0, ALU.mult, ALU.add))
                then(dve.tensor_scalar(mrow, brow, -SUPPRESS, None, ALU.mult))
                dve.tensor_copy(b_hi, mrow).then_inc(bias_rows, 1)
                dve.wait_ge(bias_rows, 1)
                dve.tensor_tensor(b_lo, mrow, as_f32(b_hi), ALU.subtract).then_inc(bias_rows, 1)
                then(dve.tensor_copy(tok[:, :], tok_i[:, :]))
                then(dve.tensor_scalar(tok_w[:, :], tok[:, :], 0.0, float(S), ALU.is_lt, ALU.mult))
                then(dve.tensor_tensor(tok[:, :], tok[:, :], tok_w[:, :], ALU.add))
                then(dve.tensor_copy(key_no, key_no_i))
                for i in range(4):
                    then(dve.tensor_scalar(hit[:, i, :], key_no, tok[:, i:i + 1], None, ALU.is_equal))
                then(dve.tensor_tensor(hit[:, 0, :], hit[:, 0, :], hit[:, 1, :], ALU.max))
                then(dve.tensor_tensor(hit[:, 2, :], hit[:, 2, :], hit[:, 3, :], ALU.max))
                then(dve.tensor_scalar(hit[:, 1, :], hit[:, 2, :], -1.0, 1.0, ALU.mult, ALU.add))
                dve.tensor_tensor(ind[0], hit[:, 0, :], hit[:, 1, :], ALU.mult).then_inc(bias_rows, 2)
                dve.tensor_copy(ind[1], hit[:, 2, :]).then_inc(bias_rows, 2)

            def rest_chunk(c, slot, count):
                dve.wait_ge(w_rounded, count)
                raw, ks = raw_chunk(c, slot)
                hi, lo = (wq_hi, wq_lo) if c < HALF else (wo_hi, wo_lo)
                for i, k in enumerate(ks):
                    if c < HALF and has_norm:
                        ins = dve.scalar_tensor_tensor(out=lo[:, k, :], in0=raw[:, i, :], scalar=nw[:, k:k + 1],
                                                       in1=as_f32(hi[:, k, :]), op0=ALU.mult, op1=ALU.subtract)
                    else:
                        ins = dve.tensor_tensor(lo[:, k, :], raw[:, i, :], as_f32(hi[:, k, :]), ALU.subtract)
                ins.then_inc(w_split, 1)

            def mean_square(n):
                dve.wait_ge(ssum_done, n + 1)
                dve.tensor_scalar(ms[:, 0, :], bank(SUMB), 1.0 / C, EPS, ALU.mult, ALU.add).then_inc(ms_step, 1)

            def invert_mean_square(n, i):
                w = S // PARTS
                if i == 0:
                    dve.wait_ge(ms_step, MS * n + 1)
                dve.reciprocal(ms[:, 1, i * w:(i + 1) * w], ms[:, 0, i * w:(i + 1) * w]).then_inc(ms_step, 1)

            def take_q(it, t, first=False):
                if has_norm:
                    dve.wait_ge(q_proj, it * T + t + 1)
                    if not first:
                        dve.wait_ge(q_lo, it * T + t)
                    dve.wait_ge(inv_done, it + 1)
                    dve.tensor_tensor(qf[:, :], bank(QB), inv[:, :], ALU.mult).then_inc(q_taken, 1)
                else:
                    dve.wait_ge(q_hi, it * T + t + 1)
                    dve.scalar_tensor_tensor(out=qn_lo[:, :], in0=bank(QB), scalar=scale, in1=as_f32(qn_hi[:, :]),
                                             op0=ALU.mult, op1=ALU.subtract).then_inc(q_lo, 1)

            def reduce_max(it, t, n):
                dve.wait_ge(smax, (it * T + t) * M + n + 1)
                col = n % QT + 32 * (n // QT)
                dve.tensor_reduce(max_cols[:, col:col + 1], bank(MAXB[n]),
                                  AX.X, ALU.max, negate=True).then_inc(reduced, 1)

            def split_x(n, c):
                dve.wait_ge(x_hi_done, n * XC + c + 1)
                dve.tensor_tensor(x_lo[:, c * XT:(c + 1) * XT, :], x_raw[:, :, :],
                                  as_f32(x_hi[:, c * XT:(c + 1) * XT, :]), ALU.subtract).then_inc(x_split, 1)

            def reciprocals(it, t, parts):
                n = S // PARTS
                for i in parts:
                    if i == 0:
                        dve.wait_ge(den_done, it * T + t + 1)
                        if not has_norm and t < 2:
                            dve.wait_ge(stored[t], 1 + it * (2 * DMA))
                        if t >= 2:
                            dve.wait_ge(o_lo, it * T + t - 1)
                    dve.reciprocal(stage[:, t % 2, i * n:(i + 1) * n], bank(DENB)[:, i * n:(i + 1) * n])\
                        .then_inc(recip_done, 1)

            def normalise(it, t):
                dve.wait_ge(recip_done, (it * T + t + 1) * PARTS)
                dve.tensor_tensor(stage[:, t % 2, :], bank(OUTB), stage[:, t % 2, :], ALU.mult).then_inc(normed, 1)

            if has_norm:
                split_x(0, 0)
                rest_chunk(0, 0, 1)
                mean_square(0)
                for i in range(PARTS):
                    invert_mean_square(0, i)
            else:
                for c in range(HALF):
                    rest_chunk(c, c % 2, c + 1)
                    if c < XC:
                        split_x(0, c)
            for t in range(AHEAD):
                take_q(0, t, first=(t == 0))
                if not has_norm and HALF + t < WCH:
                    rest_chunk(HALF + t, (HALF + t) % 2, HALF + t + 1)
            for n in range(M):
                reduce_max(0, 0, n)
            with dve.Fori(0, N) as it:
                for t in range(T):
                    for n in range(M):
                        reduce_max(*place(it, t + 1), n)
                        if has_norm and t == 0 and n == NS:
                            mean_square(it + 1)
                        if has_norm and t == 0 and n == NS + PARTS:
                            invert_mean_square(it + 1, 0)
                        if has_norm and t == 0 and n == M - 1:
                            invert_mean_square(it + 1, 1)
                            invert_mean_square(it + 1, 2)
                        if has_norm and t == 1 and n == NS:
                            invert_mean_square(it + 1, 3)
                        if t > 0 and n == 0:
                            if not has_norm:
                                reciprocals(it, t - 1, range(PARTS - 1, PARTS))
                            else:
                                normalise(it, t - 1)
                        if t > 0 and n == 1 and not has_norm:
                            normalise(it, t - 1)
                        if t == SPLIT_AT and n in XAT:
                            split_x(it + 1, XAT.index(n))
                        if has_norm and t == 0 and n == M // 2:
                            with dve.If(it % B == 0):
                                rest_chunk(1, 0, 2 * (it // B) + 2)
                        if has_norm and t == SPLIT_AT and n == M // 2 + 2:
                            with dve.If(it % B == B - 1):
                                rest_chunk(0, 0, 2 * (it // B) + 3)
                    reciprocals(it, t, range(EARLY))
                    take_q(*place(it, t + AHEAD))
                    if t < T - 1:
                        reciprocals(it, t, range(EARLY, PARTS - 1 + LATE))
                    else:
                        reciprocals(it, t, range(EARLY, PARTS))
                        normalise(it, t)
                for o in range(CK):
                    dve.wait_ge(o_proj, it * CK + o + 1)
                    dve.wait_ge(res_in[o % RS], (it * (CK // RS) + o // RS + 1) * DMA)
                    dve.wait_ge(stored[o % RES], 1 + it * (UR * DMA) + o // RES * DMA)
                    if has_norm:
                        ins = dve.tensor_tensor(results[:, o % RES, :], bank(OB[o]), x_res[:, o % RS, :], ALU.add)
                    else:
                        ins = dve.scalar_tensor_tensor(out=results[:, o % RES, :], in0=bank(OB[o]),
                                                       scalar=bo_cols[:, o:o + 1], in1=x_res[:, o % RS, :],
                                                       op0=ALU.add, op1=ALU.add)
                    ins.then_inc(added, 1)

        @block.tensor
        def _(pe):
            bank_q = q_taken if has_norm else q_lo

            def sum_squares(n):
                pe.wait_ge(sq_step, (n + 1) * SQ)
                pe.matmul(bank(SUMB), ones[:, :], sq[:, 0, :], start=True, stop=True).then_inc(ssum_done, 1)

            def project_q(it, t, tiles=range(CK), first=False):
                if t == 0 and 0 in tiles:
                    pe.wait_ge(x_split, (it + 1) * XC)
                if t == 0 and 0 in tiles and has_norm:
                    pe.wait_ge(ms_step, MS * it + 1)
                    if not first:
                        pe.wait_ge(w_split, 2 * (it // B) + 1)
                for k in tiles:
                    for i, (w, x) in enumerate(((wq_hi, x_hi), (wq_hi, x_lo), (wq_lo, x_hi))):
                        last = pe.matmul(bank(QB), w[:, k, t * P:(t + 1) * P], x[:, k, :],
                                         start=(k == 0 and i == 0), stop=(k == CK - 1 and i == 2))
                if CK - 1 in tiles:
                    last.then_inc(q_proj, 1)

            def maxima(it, t, n):
                s = t % RING
                if n == 0:
                    pe.wait_ge(k_in[s], ring_count(it, t) * (3 * DMA))
                    pe.wait_ge(q_in[s], ring_count(it, t) * (3 * H * DMA))
                elif MAXB[n] in MAXB[:n]:
                    pe.wait_ge(reduced, (it * T + t) * M + last_use(n) + 1)
                h, q = n // QT, n % QT
                for p in range(PASS):
                    last = pe.matmul(bank(MAXB[n]), q_ops[0:rows(p), s, h, p, q * P:(q + 1) * P],
                                     k_ops[0:rows(p), s, k_head(h), p, :], start=(p == 0), stop=(p == PASS - 1))
                last.then_inc(smax, 1)

            def turn(it, t):
                pe.wait_ge(reduced, (it * T + t + 1) * M)
                for q in range(QT):
                    last = pe.transpose(ps[:, TURNB, q * P:(q + 1) * P], max_cols[:, q:q + P], ident[:, :])
                last.then_inc(turned, 1)

            def scores(it, t, n):
                s, kt, hp = t % RING, n // (H // 2), n % (H // 2)
                if n == 0:
                    pe.wait_ge(shifted, it * T + t + 1)
                if n >= 2:
                    pe.wait_ge(exped, (it * T + t) * NS + n - 1)
                for j in range(2):
                    h = 2 * hp + j
                    for p in range(PASS):
                        last = pe.matmul(bank(2 * (n % 2) + j), k_ops[:, s, k_head(h), p, kt * P:(kt + 1) * P],
                                         q_ops[:, s, h, p, :], start=(p == 0), stop=(p == PASS - 1))
                last.then_inc(scored, 1)

            def outputs(it, t, kt):
                if kt == 0:
                    if kind.shared:
                        if t == 0:
                            pe.wait_ge(v_in, (it + 1) * DMA)
                    else:
                        pe.wait_ge(v_in, (it * T + t + 1) * DMA)
                    pe.wait_ge(normed, 1 + it * T + t)
                pe.wait_ge(exped, (it * T + t) * NS + (kt + 1) * (H // 2))
                for h in range(H):
                    c0 = (t if kind.shared else h) * d
                    last = pe.matmul(ps[h * d:(h + 1) * d, OUTB, :], v[:, kt, c0:c0 + d],
                                     probs[:, kt * (H // 2) + h // 2, h % 2, :],
                                     start=(kt == 0), stop=(kt == KT - 1), skip_group_check=True)
                last.then_inc(pv, 1)

            def denominators(it, t):
                pe.wait_ge(summed, (it * T + t + 1) * SUMS)
                for kt in (0, *range(min(PRE), KT)):
                    for h in (h for h in range(H) if kt == 0 or kt >= PRE[h // 2]):
                        rhs = probs[:, kt * (H // 2) + h // 2, h % 2, :] if kt else sums[:, h // 2, h % 2, :]
                        last = pe.matmul(ps[h * d:(h + 1) * d, DENB, :], ones[:, 0:d], rhs, start=(kt == 0),
                                         stop=(kt == KT - 1 or PRE[h // 2] == KT), skip_group_check=True)
                last.then_inc(den_done, 1)

            def project_out(o, tiles):
                for t in tiles:
                    for i, (w, a) in enumerate(((wo_hi, a_hi), (wo_hi, a_lo), (wo_lo, a_hi))):
                        last = pe.matmul(bank(OB[o]), w[:, t, o * P:(o + 1) * P], a[:, t, :],
                                         start=(t == 0 and i == 0), stop=(t == T - 1 and i == 2))
                if T - 1 in tiles:
                    last.then_inc(o_proj, 1)

            pe.wait_ge(consts, 2)
            pe.wait_ge(consts_v, 4)
            if has_norm:
                sum_squares(0)
                pe.wait_ge(w_split, 1)
            else:
                pe.wait_ge(w_split, HALF)
                pe.wait_ge(rows_set, 6 * DMA)
            for t in range(AHEAD):
                if t > 0:
                    pe.wait_ge(bank_q, t)
                project_q(0, t, first=(t == 0))
            for n in range(M):
                if n == 1:
                    pe.wait_ge(bank_q, AHEAD)
                maxima(0, 0, n)
            turn(0, 0)
            with pe.Fori(0, N) as it:
                for t in range(T):
                    for n in range(H // 2):
                        if t == 0 and n == 1:
                            pe.wait_ge(added, CK + it * CK)
                        scores(it, t, n)
                    if t == 0 and H == 2:
                        pe.wait_ge(added, CK + it * CK - 2)
                    for r in range(NS):
                        if has_norm and r == NS - 1:
                            outputs(it, t, KT - 1)
                        if MAXB.index(DENB) in (2 * r, 2 * r + 1):
                            pe.wait_ge(normed, 1 + it * T + t)
                        maxima(*place(it, t + 1), 2 * r)
                        summing = has_norm and t == 0 and r == NS // 2
                        if summing:
                            pe.wait_ge(reduced, (it * T + t + 1) * M + last_use(2 * r + 1) + 1)
                            sum_squares(it + 1)
                        if t == 0 and r == 0 and H == 2:
                            pe.wait_ge(added, CK + it * CK)
                        if H // 2 + r < NS and not (r == 0 and has_norm):
                            scores(it, t, H // 2 + r)
                        if r == 0:
                            pe.wait_ge(bank_q, it * T + t + AHEAD)
                        if not summing:
                            maxima(*place(it, t + 1), 2 * r + 1)
                        if r == 0 and has_norm:
                            scores(it, t, H // 2)
                        if r in OUT_AT and not (r == NS - 1 and has_norm):
                            outputs(it, t, OUT_AT.index(r))
                        if summing:
                            pe.wait_ge(ms_step, MS * (it + 1) + 1)
                            maxima(*place(it, t + 1), 2 * r + 1)
                    if not has_norm:
                        outputs(it, t, KT - 1)
                    else:
                        denominators(it, t)
                    turn(*place(it, t + 1))
                    if has_norm:
                        project_q(*place(it, t + AHEAD))
                    else:
                        project_q(*place(it, t + AHEAD), tiles=range(CK - 1))
                        denominators(it, t)
                        project_q(*place(it, t + AHEAD), tiles=range(CK - 1, CK))
                pe.wait_ge(w_split, WCH * (it // B + 1))
                pe.wait_ge(o_lo, (it + 1) * T - 1)
                pe.wait_ge(shifted, (it + 1) * T + 1)
                project_out(0, range(T - 1))
                pe.wait_ge(bank_q, (it + 1) * T + AHEAD)
                project_out(1, range(T - 1))
                pe.wait_ge(o_lo, (it + 1) * T)
                project_out(0, [T - 1])
                project_out(1, [T - 1])
                pe.wait_ge(exped, (it + 1) * (T * NS))
                for o in range(2, CK):
                    project_out(o, range(T))


def build(nc, a, out):
    k_scratch = nc.dram_tensor("k_scratch", (B, PROJ // P, 2, P, S), F32, kind="Internal").ap()
    v_scratch = nc.dram_tensor("v_scratch", (B, KT, P, PROJ), F32, kind="Internal").ap()
    project_context(nc, "kp", a["ctx_t"], a["wk"], k_scratch, True)
    project_context(nc, "vp", a["ctx_t"], a["wv"], v_scratch, False)
    bias = dict(bo=a["bo"], mask_a=a["mask_a"], mask_b=a["mask_b"], tok_a=a["tok_a"], tok_b=a["tok_b"])
    attention_layers(nc, "a0", Kind(1, INNER0, 64, False), a["x_t"], out, k_scratch, v_scratch,
                     a["wq0"], a["wo0"], bias=bias)
    attention_layers(nc, "a1", Kind(LAYERS, INNER, 32, True), out, out, k_scratch, v_scratch,
                     a["wq"], a["wo"], norm_w=a["norm_w"])


def kernel(**inputs):
    import numpy as np
    import concourse.bacc as bacc
    from concourse.bass_utils import run_bass_kernel_spmd

    own = range(1, LAYERS + 1)
    arrays = {
        "x_t": inputs["x"].transpose(0, 2, 1),
        "ctx_t": inputs["ctx_2048"].transpose(0, 2, 1),
        "wk": np.concatenate([inputs["L0_xattn_Wk"]] + [inputs[f"L{i}_xattn_wk"] for i in own], axis=1),
        "wv": np.concatenate([inputs["L0_xattn_Wv"]] + [inputs[f"L{i}_xattn_wv"] for i in own], axis=1),
        "wq0": inputs["L0_xattn_Wq"][None],
        "wo0": inputs["L0_xattn_Wo"][None],
        "wq": np.stack([inputs[f"L{i}_xattn_wq"] for i in own]),
        "wo": np.stack([inputs[f"L{i}_xattn_wo"] for i in own]),
        "norm_w": np.stack([inputs[f"L{i}_xattn_norm_w"].reshape(CK, P).T for i in own]),
        "bo": inputs["L0_xattn_bo"].reshape(CK, P).T,
        "mask_a": inputs["mask_S_fk1"],
        "mask_b": inputs["mask_S_fk0"],
        "tok_a": inputs["L0_xattn_token_indices_A"],
        "tok_b": inputs["L0_xattn_token_indices_B"],
    }
    arrays = {n: np.ascontiguousarray(x) for n, x in arrays.items()}
    nc = bacc.Bacc("TRN2", target_bir_lowering=False, num_devices=1)
    aps = {n: nc.dram_tensor(f"in_{n}", x.shape, mybir.dt.from_np(x.dtype), kind="ExternalInput").ap()
           for n, x in arrays.items()}
    out = nc.dram_tensor("out_t", (B, C, S), F32, kind="ExternalOutput").ap()
    build(nc, aps, out)
    r = run_bass_kernel_spmd(nc, [{f"in_{n}": x for n, x in arrays.items()}], core_ids=[0])
    return np.ascontiguousarray(r.results[0]["out_t"].transpose(0, 2, 1))
```
